# Optimizing a Trainium2 kernel written in Bass

```python
import numpy as np
import jax
import jax.numpy as jnp

def _softmax(x, axis=-1):
    return jax.nn.softmax(x, axis=axis)

def _gelu(x):
    return jax.nn.gelu(x, approximate=True)

def _silu(x):
    return jax.nn.silu(x)

def _sigmoid(x):
    return jax.nn.sigmoid(x)

def _layernorm(x, axis=-1, eps=1e-05):
    m = jnp.mean(x, axis=axis, keepdims=True)
    v = jnp.var(x, axis=axis, keepdims=True)
    return (x - m) / jnp.sqrt(v + eps)

def _scatter_add(tgt, idx, src, axis=0):
    return tgt.at[idx].add(src)

def _segment_sum(src, seg, n):
    return jax.ops.segment_sum(src, seg, n)
kernel_name = 'mk_adj_preln_d1_adj_r2_c8da03'

def setup_inputs(seed: int=0):
    np.random.seed(seed)
    _w = jnp.asarray

    def _rec_inputs():
        import jax
        import jax.numpy as jnp
        _gk = jax.random.key(seed)
        x = -0.006082 + 1.001 * jax.random.normal(jax.random.fold_in(_gk, 1), (8192, 64), jnp.float32)
        _a = jax.random.bernoulli(jax.random.fold_in(_gk, 2), 0.000488281, (8192, 8192))
        adj = _a.astype(jnp.int32)
        return (x, adj)
    x, adj = _rec_inputs()

    def _L0_gnn_setup():
        import jax, jax.numpy as jnp
        import numpy as np
        ALPHA = 0.2
        NEG_INF = -9000000000000000.0
        key = jax.random.key(seed)
        k1, k2, k3, k4 = jax.random.split(key, 4)
        N, F_IN, F_OUT = (512, 64, 64)
        h = jax.random.normal(k1, (N, F_IN), dtype=jnp.float32)
        adj = jax.random.randint(k2, (N, N), 0, 2, dtype=jnp.int32)
        lim_W = 1.414 * np.sqrt(6.0 / (F_IN + F_OUT))
        W = jax.random.uniform(k3, (F_IN, F_OUT), minval=-lim_W, maxval=lim_W, dtype=jnp.float32)
        lim_a = 1.414 * np.sqrt(6.0 / (2 * F_OUT + 1))
        a = jax.random.uniform(k4, (2 * F_OUT, 1), minval=-lim_a, maxval=lim_a, dtype=jnp.float32)
        return {'h': h, 'adj': adj, 'W': W, 'a': a}
    _L0_gnn_all = _L0_gnn_setup()
    _L0_gnn_in = {k: v for k, v in _L0_gnn_all.items() if k in ('W', 'a')}
    del _L0_gnn_all
    return {'x': x, 'adj': adj, 'L0_gnn_W': _L0_gnn_in['W'], 'L0_gnn_a': _L0_gnn_in['a']}

def reference(x, adj, L0_gnn_W, L0_gnn_a):
    import jax
    import jax.numpy as jnp

    def _L0_gnn_ref(h, adj, W, a):
        import jax, jax.numpy as jnp
        import numpy as np
        ALPHA = 0.2
        NEG_INF = -9000000000000000.0
        F_OUT = W.shape[1]
        Wh = h @ W
        a1, a2 = (a[:F_OUT, 0], a[F_OUT:, 0])
        e = (Wh @ a1)[:, None] + (Wh @ a2)[None, :]
        e = jax.nn.leaky_relu(e, negative_slope=ALPHA)
        scores = jnp.where(adj > 0, e, jnp.float32(NEG_INF))
        attention = jax.nn.softmax(scores, axis=1)
        h_prime = attention @ Wh
        return jax.nn.elu(h_prime)
    h = jnp.maximum(_layernorm(x, axis=-1), 0.0)
    x = x + _L0_gnn_ref(h, adj, L0_gnn_W, L0_gnn_a)
    return x

_drawn_inputs = setup_inputs


def setup_inputs(seed=0):
    import zlib

    import numpy as np

    out = dict(_drawn_inputs(seed))
    spreads = {}
    factors = {}
    for name, (base, spread) in spreads.items():
        noise = np.random.default_rng([zlib.crc32(name.encode()), seed]).standard_normal(out[name].shape)
        drawn = base * np.exp(spread * noise) if base else spread * noise
        out[name] = jnp.asarray(drawn.astype(out[name].dtype))
    for name, factor in factors.items():
        out[name] = (out[name] * factor).astype(out[name].dtype)
    return out
```

```python
from contextlib import ExitStack

import concourse.bass as bass
from concourse import mybir

ALU = mybir.AluOpType
ACT = mybir.ActivationFunctionType
AX = mybir.AxisListType
F32 = mybir.dt.float32
BF16 = mybir.dt.bfloat16
F16 = mybir.dt.float16
I32 = mybir.dt.int32

P = 128
ALPHA = 0.2
EPS = 1e-5
BIG = 2.0 ** 40
TOP = 2.0 ** 15


def build_gat(nc, x, adj, W, a, out):
    N, F = x.shape
    FE = F + 1
    FX = F + 2
    FP = 2 * FE
    JB = N // P
    K = 4
    G = JB // K
    WI = P * K
    E = 2
    WU = E * WI
    UC = 2
    CJ = UC * E * P
    RC = 4
    RU = 4
    BU = RC * UC
    QG = JB // (BU * E)
    LEAD = RU - 1
    LNP = 2
    assert JB % (BU * E) == 0 and JB % K == 0 and BU % RU == 0 and 2 * F <= P

    ctx = ExitStack()
    with ctx:
        def sb(name, shape, dt=F32):
            return ctx.enter_context(nc.sbuf_tensor(name, shape, dt))

        def sem(name):
            return ctx.enter_context(nc.semaphore(name))

        adj_ring = sb("adj_ring", [P, RC, K, CJ], I32)
        san = sb("san", [P, RC, K, CJ], BF16)
        srow = sb("srow", [P, N])
        Wh = sb("Wh", [P, JB, FX])
        V = sb("V", [P, JB, 3 * FP], F16)
        rings = sb("rings", [P, 2 * RU + BU, WU], BF16)
        mask = rings[:, 0:RU]
        up = rings[:, RU:2 * RU]
        step = rings[:, 2 * RU:2 * RU + BU]
        hT = V[0:F, :, :].rearrange("p j v -> p (j v)")[:, 0:2 * N].bitcast(F32)
        flat = rings[:, :, :].rearrange("p r w -> p (r w)").bitcast(F32)
        xh = flat[:, 0:JB * F].rearrange("p (r f) -> p r f", f=F)
        sq = san[:, :, :, :].rearrange("p s k j -> p (s k j)").bitcast(F32).rearrange("p (r f) -> p r f", f=F)
        NR = 4
        RR = JB // NR
        Y = flat[:, 0:4 * RR * FE].rearrange("p (b h r f) -> p b h r f", b=2, h=2, f=FE)
        ident = sb("ident", [P, P])
        identb = sb("identb", [P, P], BF16)
        ones = sb("ones", [P, P])
        zerob = sb("zerob", [P, 2 * FP], BF16)
        WT = sb("WT", [F, F])
        WT2 = sb("WT2", [F, F])
        Wx = sb("Wx", [F, FX])
        a_sb = sb("a_sb", [F, 2])
        eps = sb("eps", [P, 1])
        stat = sb("stat", [P, 5, JB])
        ext = sb("ext", [P, 3])
        norm2 = sb("norm2", [F, 1])
        ext2 = sb("ext2", [3, 1])
        extd = sb("extd", [3, 3])
        lim = sb("lim", [P, 8])
        uu = sb("uu", [P, 4, JB])
        nt = sb("nt", [P, JB])
        bt = sb("bt", [P, JB])
        yy = sb("yy", [P, JB, 2])
        ab = sb("ab", [P, JB, 2])
        tree = sb("tree", [P, JB // 2, F])
        tot = sb("tot", [P, FE])
        acc_sb = sb("acc_sb", [P, K, 2 * FP])
        xg = sb("xg", [P, K, F])
        parts = sb("parts", [P, K, 2, FE])
        sums = sb("sums", [P, K, FE])
        fixd = sb("fixd", [P, K, FE])
        lone = sb("lone", [P, K])
        rden = sb("rden", [P, K])
        hp = sb("hp", [P, K, F])
        neg = sb("neg", [P, K, F])
        res = sb("res", [P, K, F])

        psum = ctx.enter_context(nc.psum_tensor("psum", [P, 8, 512], F32))
        adjT = [psum[:, s, :].bitcast(BF16) for s in range(RU)]
        acc = [psum[:, 4 + k, 0:2 * FP] for k in range(K)]
        total_ps = psum[:, 4, 2 * FP:2 * FP + F]
        half = [psum[:, 0:4, :], psum[:, 4:8, :]]

        s_x = [sem(f"x_loaded_{b}") for b in range(LNP)]
        s_w = sem("weights_loaded")
        s_id0 = sem("identity_cleared")
        s_const = sem("constants_made")
        s_sum = sem("sum_ready")
        s_nm = sem("minus_mean_ready")
        s_xc = sem("centred")
        s_sq = sem("squares_ready")
        s_var = sem("variance_ready")
        s_std = sem("deviation_ready")
        s_rstd = sem("reciprocal_ready")
        s_h = sem("h_ready")
        s_wp = sem("weight_product")
        s_wt = sem("weight_transposed")
        s_wx = sem("weights_extended")
        s_round = sem("round_in_psum")
        s_even = sem("even_round_copied")
        s_odd = sem("odd_round_copied")
        s_ext = sem("extrema_step")
        s_extp = sem("extrema_product")
        s_lim = sem("limits_ready")
        s_norm = sem("norms_of_W_step")
        s_sq2 = sem("bound_ready")
        s_u = sem("u_written")
        s_us = sem("u_scaled")
        s_small = sem("small_columns_ready")
        s_yy = sem("exponents_ready")
        s_ab = sem("alpha_beta_ready")
        s_Y = [sem(f"Y_{h}_ready") for h in range(2)]
        s_hi = [sem(f"high_{h}_ready") for h in range(2)]
        s_lo = [sem(f"low_{h}_ready") for h in range(2)]
        s_V = sem("V_negated")
        s_tree = sem("tree_step")

        s_adj = [sem(f"adj_loaded_{s}") for s in range(RC)]
        s_san = [sem(f"chunk_sanitized_{s}") for s in range(RC)]
        s_T = [sem(f"unit_transposed_{u}") for u in range(BU)]
        s_mask = sem("masks_written")
        s_stepA = sem("steps_written_by_ScalarE")
        s_stepV = sem("steps_written_by_VectorE")
        s_up = sem("ups_written")
        s_P = [sem(f"unit_multiplied_{u}") for u in range(RU)]
        s_group = sem("groups_summed")
        s_evac = sem("acc_banks_copied")
        s_accsb = sem("acc_sb_written")
        s_tot = sem("total_copied")
        s_xg = sem("xg_loaded")
        s_fix = sem("pool_step")
        s_rden = sem("denominators_inverted")
        s_neg = sem("negative_part_ready")
        s_exp = sem("exp_ready")
        s_res = sem("result_ready")
        s_out = sem("out_stored")

        ONE = 1
        STEPS = 9

        adj_v = adj.rearrange("(g k p) j -> g p k j", p=P, k=K)
        x_v = x.rearrange("(g k p) f -> g p k f", p=P, k=K)
        out_v = out.rearrange("(g k p) f -> g p k f", p=P, k=K)
        RB = JB // LNP

        def hT_round(r):
            dst = hT.rearrange("f (p j) -> f j p", p=P)[:, r * RR:(r + 1) * RR, :]
            return dst, half[r % 2][0:F].rearrange("f b (j p) -> f (b j) p", p=P)

        def Wh_round(r):
            dst = Wh[:, r * RR:(r + 1) * RR, :].rearrange("p (b j) f -> p b (j f)", b=4)
            return dst, half[r % 2][:, :, 0:RR // 4 * FX]

        def srow_round(r):
            return srow[:, r * RR * P:(r + 1) * RR * P].rearrange("q (b w) -> q b w", b=4), half[r % 2]

        block = ctx.enter_context(nc.Block())

        @block.sync
        def _(sp):
            xs = x.rearrange("(p r) f -> p r f", p=P)
            for b in range(LNP):
                sp.dma_start(xh[:, b * RB:(b + 1) * RB, :], xs[:, b * RB:(b + 1) * RB, :]).then_inc(s_x[b], 16)
            with sp.Fori(0, G) as g:
                with sp.Fori(0, QG) as q:
                    for s in range(RC):
                        sp.wait_ge(s_san[s], ONE + g * QG + q)
                        sp.dma_start(adj_ring[:, s], adj_v[g, :, :, bass.ds((q * RC + s) * CJ, CJ)])\
                            .then_inc(s_adj[s], 16)

        @block.gpsimd
        def _(pool):
            pool.sem_inc(s_fix, ONE)
            nc.gpsimd.memset(ident[:, :], 0.0).then_inc(s_id0, 1)
            nc.gpsimd.memset(identb[:, :], 0.0).then_inc(s_id0, 1)
            nc.gpsimd.memset(ones[:, :], 1.0).then_inc(s_const, 1)
            nc.gpsimd.memset(zerob[:, :], 0.0).then_inc(s_const, 1)
            nc.gpsimd.memset(eps[:, :], EPS).then_inc(s_const, 1)
            nc.gpsimd.memset(tot[:, F:FE], float(N)).then_inc(s_const, 1)
            nc.gpsimd.memset(ext[:, 2:3], 0.0).then_inc(s_const, 1)
            pool.wait_ge(s_id0, 2)
            for m in (ident, identb):
                nc.gpsimd.affine_select(out=m[:, :], in_=m[:, :], compare_op=ALU.not_equal, fill=1.0, base=0,
                                        pattern=[[-1, P]], channel_multiplier=1).then_inc(s_const, 1)
            pool.wait_ge(s_us, 1)
            for r in (1, 3):
                b = slice(r * RR, (r + 1) * RR)
                if r == 3:
                    for h in range(2):
                        pool.wait_ge(s_lo[h], r - 1)
                for h in range(2):
                    nc.gpsimd.tensor_tensor(Y[:, 1, h, :, 0:F], Wh[:, b, 0:F],
                                            uu[:, 2 + h, b].unsqueeze(2).to_broadcast([P, RR, F]),
                                            ALU.mult)
                    nc.gpsimd.tensor_copy(Y[:, 1, h, :, F], uu[:, 2 + h, b]).then_inc(s_Y[1], 1)
            nc.gpsimd.tensor_tensor(tree[:, :, :], Wh[:, 0:JB // 2, 0:F], Wh[:, JB // 2:JB, 0:F],
                                    ALU.add).then_inc(s_tree, 1)
            w, n = JB // 4, 1
            while w >= 1:
                pool.wait_ge(s_tree, n)
                nc.gpsimd.tensor_tensor(tree[:, 0:w, :], tree[:, 0:w, :], tree[:, w:2 * w, :],
                                        ALU.add).then_inc(s_tree, 1)
                w, n = w // 2, n + 1
            pool.wait_ge(s_ab, 1)
            for g in range(G):

                def after(k):
                    pool.wait_ge(s_fix, ONE + g * STEPS + k)

                pool.dma_start(xg[:, :, :], x_v[g]).then_inc(s_xg, 16)
                pool.wait_ge(s_accsb, g + 1)
                acc_v = acc_sb[:, :, :].rearrange("p k (s h f) -> p (k s) h f", h=2, f=FE)
                nc.gpsimd.tensor_tensor(parts[:, :, :, :].rearrange("p k s f -> p (k s) f"), acc_v[:, :, 0],
                                        acc_v[:, :, 1], ALU.add).then_inc(s_fix, 1)
                after(1)
                nc.gpsimd.tensor_tensor(parts[:, :, :, :].rearrange("p k s f -> p (k s) f"),
                                        parts[:, :, :, :].rearrange("p k s f -> p (k s) f"),
                                        ab[:, g * K:(g + 1) * K, :].rearrange("p k s -> p (k s)").unsqueeze(2)
                                        .to_broadcast([P, 2 * K, FE]), ALU.mult).then_inc(s_fix, 1)
                after(2)
                nc.gpsimd.tensor_tensor(sums[:, :, :], parts[:, :, 0], parts[:, :, 1], ALU.add).then_inc(s_fix, 1)
                after(3)
                nc.gpsimd.tensor_scalar(lone[:, :], sums[:, :, F], 0.0, None, ALU.is_equal).then_inc(s_fix, 1)
                after(4)
                nc.gpsimd.tensor_tensor(fixd[:, :, :], lone[:, :].unsqueeze(2).to_broadcast([P, K, FE]),
                                        tot[:, :].unsqueeze(1).to_broadcast([P, K, FE]), ALU.mult).then_inc(s_fix, 1)
                after(5)
                nc.gpsimd.tensor_tensor(fixd[:, :, :], fixd[:, :, :], sums[:, :, :], ALU.add).then_inc(s_fix, 1)
                pool.wait_ge(s_rden, g + 1)
                nc.gpsimd.tensor_tensor(hp[:, :, :], fixd[:, :, 0:F], rden[:, :].unsqueeze(2).to_broadcast([P, K, F]),
                                        ALU.mult).then_inc(s_fix, 1)
                after(7)
                nc.gpsimd.tensor_scalar(neg[:, :, :], hp[:, :, :], 0.0, None, ALU.min).then_inc(s_neg, 1)
                nc.gpsimd.tensor_scalar(hp[:, :, :], hp[:, :, :], 0.0, -1.0, ALU.max, ALU.add).then_inc(s_fix, 1)
                after(8)
                pool.wait_ge(s_xg, 16 * g + 16)
                nc.gpsimd.tensor_tensor(hp[:, :, :], hp[:, :, :], xg[:, :, :], ALU.add).then_inc(s_fix, 1)
                after(STEPS)
                pool.wait_ge(s_exp, g + 1)
                if g:
                    pool.wait_ge(s_out, 16 * g)
                nc.gpsimd.tensor_tensor(res[:, :, :], hp[:, :, :], neg[:, :, :], ALU.add).then_inc(s_res, 1)
                pool.wait_ge(s_res, g + 1)
                pool.dma_start(out_v[g], res[:, :, :]).then_inc(s_out, 16)
            pool.wait_ge(s_out, 16 * G)

        @block.scalar
        def _(act):
            for v in s_san:
                act.sem_inc(v, ONE)
            act.sem_inc(s_evac, K)
            act.dma_start(Wx[:, 0:F], W).then_inc(s_w, 16)
            with nc.allow_non_contiguous_dma(reason="128 numbers"):
                act.dma_start(a_sb[:, :], a.rearrange("(c f) o -> f (c o)", c=2)).then_inc(s_w, 16)
            act.wait_ge(s_wp, 1)
            nc.scalar.activation(WT[:, :], psum[0:F, 7, 0:F], ACT.Copy).then_inc(s_wt, 1)
            act.wait_ge(s_wp, 2)
            nc.scalar.activation(Wx[:, F:FX], psum[0:F, 7, F:FX], ACT.Copy).then_inc(s_wx, 1)
            for b in range(LNP):
                r = slice(b * RB, (b + 1) * RB)
                act.wait_ge(s_xc, b + 1)
                nc.scalar.activation(sq[:, r], xh[:, r], ACT.Square).then_inc(s_sq, 1)
            act.wait_ge(s_const, 7)
            for b in range(LNP):
                r = slice(b * RB, (b + 1) * RB)
                act.wait_ge(s_var, b + 1)
                nc.scalar.activation(stat[:, 3, r], stat[:, 2, r], ACT.Sqrt, bias=eps[:, :],
                                     scale=1.0 / F).then_inc(s_std, 1)
            act.wait_ge(s_norm, 2)
            nc.scalar.activation(ext[0:F, 2:3], norm2[:, :], ACT.Sqrt, scale=float(F)).then_inc(s_sq2, 1)
            for r in (1, 3):
                act.wait_ge(s_round, r + 1)
                nc.scalar.activation(*hT_round(r), ACT.Copy).then_inc(s_odd, 1)
            for r in (1, 3):
                act.wait_ge(s_round, NR + r + 1)
                nc.scalar.activation(*Wh_round(r), ACT.Copy).then_inc(s_odd, 1)
            act.wait_ge(s_lim, 1)
            t_all = Wh[:, :, F + 1]
            nc.scalar.activation(uu[:, 0], t_all, ACT.Exp, bias=lim[:, 3:4]).then_inc(s_u, 1)
            nc.scalar.activation(uu[:, 1], t_all, ACT.Exp, bias=lim[:, 4:5], scale=ALPHA).then_inc(s_u, 1)
            nc.scalar.activation(bt[:, :], t_all, ACT.Copy, scale=BIG).then_inc(s_small, 1)
            act.wait_ge(s_yy, 2)
            nc.scalar.activation(ab[:, :, :], yy[:, :, :], ACT.Exp).then_inc(s_ab, 1)
            for r in range(NR):
                for h in range(2):
                    b = slice(r * RR, (r + 1) * RR)
                    act.wait_ge(s_Y[r % 2], r // 2 * 2 + h + 1)
                    nc.scalar.activation(V[:, b, 2 * h * FP:2 * h * FP + FE], Y[:, r % 2, h], ACT.Copy)\
                        .then_inc(s_hi[h], 1)
                if r % 2:
                    act.wait_ge(s_round, 2 * NR + r + 1)
                    nc.scalar.activation(*srow_round(r), ACT.Copy).then_inc(s_odd, 1)

            def prepare(m, g, q):
                for s in range(RC):
                    u = UC * s
                    act.wait_ge(s_up, m * BU + u + 1)
                    act.wait_ge(s_adj[s], 16 * m + 16)
                    act.wait_ge(s_T[UC * s + UC - 1], ONE + m)
                    nc.scalar.activation(san[:, s], adj_ring[:, s], ACT.Relu).then_inc(s_san[s], 1)
                    for e in range(E):
                        last = nc.scalar.activation(step[:, u, e * WI:(e + 1) * WI], srow[:, bass.ds(g * WI, WI)],
                                                    ACT.Relu, bias=bt[:, bass.ds(q * BU * E + u * E + e, 1)],
                                                    scale=BIG)
                    last.then_inc(s_stepA, 1)

            def copy_sums(g):
                act.wait_ge(s_group, g + 1)
                act.wait_ge(s_fix, ONE + g * STEPS)
                nc.scalar.activation(tot[:, 0:F], total_ps, ACT.Copy).then_inc(s_tot, 1)
                for k in range(K):
                    nc.scalar.activation(acc_sb[:, k], acc[k], ACT.Copy).then_inc(s_evac, 1)
                act.wait_ge(s_evac, K + (g + 1) * K)
                act.wait_ge(s_tot, g + 1)
                act.sem_inc(s_accsb, 1)

            def exp_part(g):
                act.wait_ge(s_neg, g + 1)
                nc.scalar.activation(neg[:, :, :], neg[:, :, :], ACT.Exp).then_inc(s_exp, 1)

            act.wait_ge(s_even, 6)
            act.wait_ge(s_odd, 6)
            act.wait_ge(s_var, LNP)
            act.wait_ge(s_small, 1)
            act.wait_ge(s_lo[0], NR)
            act.wait_ge(s_lo[1], NR)
            with act.Fori(0, QG) as q:
                prepare(q, 0, q)
            with act.Fori(0, G - 1) as g:
                prepare((g + 1) * QG, g + 1, 0)
                copy_sums(g)
                prepare((g + 1) * QG + 1, g + 1, 1)
                prepare((g + 1) * QG + 2, g + 1, 2)
                exp_part(g)
                prepare((g + 1) * QG + 3, g + 1, 3)
            copy_sums(G - 1)
            exp_part(G - 1)

        @block.vector
        def _(dve):
            dve.sem_inc(s_mask, RU)
            dve.sem_inc(s_up, BU)
            dve.wait_ge(s_wt, 1)
            nc.vector.tensor_tensor(WT2[:, :], WT[:, :], WT[:, :], ALU.mult).then_inc(s_norm, 1)
            dve.wait_ge(s_norm, 1)
            nc.vector.reduce_sum(norm2[:, :], WT2[:, :], axis=AX.X).then_inc(s_norm, 1)
            for b in range(LNP):
                r = slice(b * RB, (b + 1) * RB)
                dve.wait_ge(s_x[b], 16)
                nc.vector.reduce_sum(stat[:, 0, r], xh[:, r], axis=AX.X).then_inc(s_sum, 1)
                dve.wait_ge(s_sum, b + 1)
                nc.vector.tensor_scalar(stat[:, 1, r], stat[:, 0, r], -1.0 / F, None, ALU.mult).then_inc(s_nm, 1)
                dve.wait_ge(s_nm, b + 1)
                nc.vector.tensor_tensor(xh[:, r], xh[:, r], stat[:, 1, r].unsqueeze(2).to_broadcast([P, RB, F]),
                                        ALU.add).then_inc(s_xc, 1)
            for b in range(LNP):
                r = slice(b * RB, (b + 1) * RB)
                dve.wait_ge(s_sq, b + 1)
                nc.vector.reduce_sum(stat[:, 2, r], sq[:, r], axis=AX.X).then_inc(s_var, 1)
            for b in range(LNP):
                r = slice(b * RB, (b + 1) * RB)
                dve.wait_ge(s_std, b + 1)
                nc.vector.reciprocal(stat[:, 4, r], stat[:, 3, r]).then_inc(s_rstd, 1)
                dve.wait_ge(s_rstd, b + 1)
                nc.vector.scalar_tensor_tensor(out=xh[:, r], in0=xh[:, r], scalar=0.0,
                                               in1=stat[:, 4, r].unsqueeze(2).to_broadcast([P, RB, F]),
                                               op0=ALU.max, op1=ALU.mult).then_inc(s_h, 1)
            for r in (0, 2):
                dve.wait_ge(s_round, r + 1)
                nc.vector.tensor_copy(*hT_round(r)).then_inc(s_even, 1)
            for r in (0, 2):
                dve.wait_ge(s_round, NR + r + 1)
                nc.vector.tensor_copy(*Wh_round(r)).then_inc(s_even, 1)
            dve.wait_ge(s_even, 4)
            dve.wait_ge(s_odd, 4)
            t_all = Wh[:, :, F + 1]
            nc.vector.tensor_reduce(ext[:, 0:1], t_all, AX.X, ALU.max).then_inc(s_ext, 1)
            nc.vector.tensor_reduce(ext[:, 1:2], t_all, AX.X, ALU.min).then_inc(s_ext, 1)
            dve.wait_ge(s_ext, 2)
            nc.vector.tensor_scalar(ext[:, 1:2], ext[:, 1:2], -1.0, None, ALU.mult).then_inc(s_ext, 1)
            dve.wait_ge(s_extp, 1)
            nc.vector.tensor_reduce(ext2[:, 0:1], psum[0:3, 0, 0:P], AX.X, ALU.max).then_inc(s_ext, 1)
            dve.wait_ge(s_ext, 4)
            nc.vector.tensor_scalar(extd[:, :], ident[0:3, 0:3], ext2[:, 0:1], None, ALU.mult).then_inc(s_ext, 1)
            dve.wait_ge(s_extp, 2)
            nc.vector.tensor_copy(lim[:, 0:3], psum[:, 0, P:P + 3]).then_inc(s_ext, 1)
            dve.wait_ge(s_ext, 6)
            nc.vector.tensor_scalar(lim[:, 3:4], lim[:, 0:1], -1.0, None, ALU.mult)
            nc.vector.tensor_scalar(lim[:, 4:5], lim[:, 0:1], -ALPHA, None, ALU.mult)
            nc.vector.tensor_scalar(lim[:, 5:6], lim[:, 2:3], 1.0, 1.0 / TOP, ALU.max, ALU.mult).then_inc(s_lim, 1)
            dve.wait_ge(s_lim, 1)
            nc.vector.reciprocal(lim[:, 6:7], lim[:, 5:6]).then_inc(s_lim, 1)
            s_all = Wh[:, :, F]
            nc.vector.tensor_scalar(yy[:, :, 0], s_all, lim[:, 0:1], 1 - ALPHA, ALU.add, ALU.mult).then_inc(s_yy, 1)
            dve.wait_ge(s_yy, 1)
            nc.vector.tensor_scalar(yy[:, :, 1], yy[:, :, 0], -1.0, 0.0, ALU.mult, ALU.min).then_inc(s_ext, 1)
            dve.wait_ge(s_ext, 7)
            nc.vector.tensor_scalar(yy[:, :, 0], yy[:, :, 0], 0.0, None, ALU.min).then_inc(s_yy, 1)
            nc.vector.tensor_scalar(nt[:, :], Wh[:, :, F + 1], -1.0, None, ALU.mult).then_inc(s_ext, 1)
            dve.wait_ge(s_u, 2)
            dve.wait_ge(s_lim, 2)
            nc.vector.tensor_scalar(uu[:, 2:4], uu[:, 0:2], lim[:, 6:7], None, ALU.mult).then_inc(s_us, 1)
            dve.wait_ge(s_us, 1)
            for r in range(NR):
                b = slice(r * RR, (r + 1) * RR)
                if r % 2 == 0:
                    if r:
                        for h in range(2):
                            dve.wait_ge(s_lo[h], r - 1)
                    for h in range(2):
                        nc.vector.tensor_tensor(Y[:, 0, h, :, 0:F], Wh[:, b, 0:F],
                                                uu[:, 2 + h, b].unsqueeze(2).to_broadcast([P, RR, F]), ALU.mult)
                        nc.vector.tensor_copy(Y[:, 0, h, :, F], uu[:, 2 + h, b]).then_inc(s_Y[0], 1)
                for h in range(2):
                    o = 2 * h * FP
                    dve.wait_ge(s_hi[h], r + 1)
                    nc.vector.tensor_tensor(V[:, b, o + FE:o + FP], Y[:, r % 2, h], V[:, b, o:o + FE],
                                            ALU.subtract).then_inc(s_lo[h], 1)
                dve.wait_ge(s_lo[1], r + 1)
                nc.vector.tensor_scalar(V[:, b, FP:2 * FP], V[:, b, 2 * FP:3 * FP], -1.0, None,
                                        ALU.mult).then_inc(s_V, 1)
                if r % 2 == 0:
                    dve.wait_ge(s_round, 2 * NR + r + 1)
                    nc.vector.tensor_copy(*srow_round(r)).then_inc(s_even, 1)
            dve.wait_ge(s_even, 6)
            dve.wait_ge(s_odd, 6)
            dve.wait_ge(s_ext, 8)
            dve.wait_ge(s_V, NR)

            def take_up(m, u):
                dve.wait_ge(s_mask, RU + m * BU + u + 1)
                dve.wait_ge(s_stepV if u % 2 else s_stepA, m * (BU // 2) + u // 2 + 1)
                nc.vector.tensor_tensor(up[:, u % RU], mask[:, u % RU], step[:, u], ALU.min).then_inc(s_up, 1)

            def masks(g, first, bodies):
                with dve.Fori(first, first + bodies) as q:
                    m = g * QG + q
                    for u in range(BU):
                        dve.wait_ge(s_T[u], ONE + m + 1)
                        dve.wait_ge(s_P[u % RU], ONE + m * (BU // RU) + u // RU)
                        nc.vector.tensor_scalar(mask[:, u % RU], adjT[u % RU], 0.0, None, ALU.is_gt)\
                            .then_inc(s_mask, 1)
                        if u % 2:
                            dve.wait_ge(s_up, m * BU + u + 1)
                            for e in range(E):
                                last = nc.vector.tensor_scalar(step[:, u, e * WI:(e + 1) * WI],
                                                               srow[:, bass.ds(g * WI, WI)],
                                                               nt[:, bass.ds(q * BU * E + u * E + e, 1)], None,
                                                               ALU.is_ge)
                            last.then_inc(s_stepV, 1)
                        if u:
                            take_up(m, u - 1)
                    take_up(m, BU - 1)

            def invert(g):
                dve.wait_ge(s_fix, ONE + g * STEPS + 6)
                nc.vector.reciprocal(rden[:, :], fixd[:, :, F]).then_inc(s_rden, 1)

            masks(0, 0, QG)
            with dve.Fori(0, G - 1) as g:
                masks(g + 1, 0, 2)
                invert(g)
                masks(g + 1, 2, QG - 2)
            invert(G - 1)

        @block.tensor
        def _(pe):
            for v in s_T + s_P:
                pe.sem_inc(v, ONE)
            pe.wait_ge(s_w, 32)
            pe.wait_ge(s_const, 7)
            nc.tensor.transpose(psum[0:F, 7, 0:F], Wx[:, 0:F], ident[0:F, 0:F]).then_inc(s_wp, 1)
            pe.wait_ge(s_wt, 1)
            nc.tensor.matmul(psum[0:F, 7, F:FX], WT[:, :], a_sb[:, :], start=True, stop=True).then_inc(s_wp, 1)
            for r in range(NR):
                pe.wait_ge(s_h, r * RR // RB + 1)
                if r == 1:
                    pe.wait_ge(s_wx, 1)
                if r >= 2:
                    pe.wait_ge(s_even if r % 2 == 0 else s_odd, r // 2)
                for j in range(RR):
                    last = nc.tensor.transpose(half[r % 2][0:F, j // 4, (j % 4) * P:(j % 4 + 1) * P],
                                               xh[:, r * RR + j, :], ident[:, :])
                last.then_inc(s_round, 1)
            pe.wait_ge(s_even, 2)
            pe.wait_ge(s_odd, 2)
            for r in range(NR):
                if r >= 2:
                    pe.wait_ge(s_even if r % 2 == 0 else s_odd, 2 + r // 2)
                for j in range(RR):
                    jb = r * RR + j
                    last = nc.tensor.matmul(half[r % 2][:, j // 4, (j % 4) * FX:(j % 4 + 1) * FX],
                                            hT[:, jb * P:(jb + 1) * P], Wx[:, :], start=True, stop=True)
                last.then_inc(s_round, 1)
            pe.wait_ge(s_ext, 3)
            pe.wait_ge(s_sq2, 1)
            nc.tensor.transpose(psum[0:3, 0, 0:P], ext[:, :], ident[:, :]).then_inc(s_extp, 1)
            pe.wait_ge(s_ext, 5)
            nc.tensor.matmul(psum[:, 0, P:P + 3], ones[0:3, :], extd[:, :], start=True, stop=True).then_inc(s_extp, 1)
            pe.wait_ge(s_lim, 1)
            for r in range(NR):
                if r >= 2:
                    pe.wait_ge(s_even if r % 2 == 0 else s_odd, 4 + r // 2)
                for j in range(RR):
                    jb = r * RR + j
                    last = nc.tensor.transpose(half[r % 2][:, j // 4, (j % 4) * P:(j % 4 + 1) * P],
                                               Wh[:, jb, F:F + 1].to_broadcast([P, P]), ident[:, :])
                last.then_inc(s_round, 1)

            def transpose_unit(m, u):
                if u % UC == 0:
                    pe.wait_ge(s_san[u // UC], ONE + m + 1)
                pe.wait_ge(s_mask, m * BU + u + 1)
                for e in range(E):
                    for k in range(K):
                        c = (u % UC) * E + e
                        b = e * K + k
                        last = nc.tensor.transpose(adjT[u % RU][:, b * P:(b + 1) * P],
                                                   san[:, u // UC, k, c * P:(c + 1) * P], identb[:, :])
                last.then_inc(s_T[u], 1)

            def multiply_unit(m, u, q):
                pe.wait_ge(s_up, BU + m * BU + u + 1)
                for e in range(E):
                    v = V[:, bass.ds(q * BU * E + u * E + e, 1), :].rearrange("p o v -> p (o v)")
                    for k in range(K):
                        b = e * K + k
                        nc.tensor.matmul(acc[k][:, FP:2 * FP], mask[:, u % RU, b * P:(b + 1) * P],
                                         v[:, 2 * FP:3 * FP], start=False, stop=False, skip_group_check=True)
                        last = nc.tensor.matmul(acc[k], up[:, u % RU, b * P:(b + 1) * P], v[:, 0:2 * FP],
                                                start=False, stop=False, skip_group_check=True)
                last.then_inc(s_P[u % RU], 1)

            def body(m, q, last=False):
                for u in range(BU):
                    if u + LEAD < BU:
                        transpose_unit(m, u + LEAD)
                    elif not last:
                        transpose_unit(m + 1, u + LEAD - BU)
                    multiply_unit(m, u, q)

            def open_group(g):
                for k in range(K):
                    pe.wait_ge(s_evac, g * K + k + 1)
                    nc.tensor.matmul(acc[k], identb[:, :], zerob[:, :], start=True, stop=False,
                                     skip_group_check=True)

            def close_group():
                nc.tensor.matmul(total_ps, ones[:, :], tree[:, 0, :], start=False, stop=True,
                                 skip_group_check=True).then_inc(s_group, 1)

            pe.wait_ge(s_even, 6)
            pe.wait_ge(s_odd, 6)
            for u in range(LEAD):
                transpose_unit(0, u)
            pe.wait_ge(s_V, NR)
            pe.wait_ge(s_tree, 6)
            with pe.Fori(0, G - 1) as g:
                open_group(g)
                with pe.Fori(0, QG) as q:
                    body(g * QG + q, q)
                close_group()
            open_group(G - 1)
            with pe.Fori(0, QG - 1) as q:
                body((G - 1) * QG + q, q)
            body(G * QG - 1, QG - 1, last=True)
            close_group()


_INS = ["x", "adj", "L0_gnn_W", "L0_gnn_a"]


def kernel(**inputs):
    import numpy as np
    import concourse.bacc as bacc
    from concourse.bass_utils import run_bass_kernel_spmd

    nc = bacc.Bacc("TRN2", target_bir_lowering=False, num_devices=1)
    arrays, args = {}, []
    for name in _INS:
        v = np.ascontiguousarray(inputs[name])
        arrays[f"in_{name}"] = v
        args.append(nc.dram_tensor(f"in_{name}", v.shape, mybir.dt.from_np(v.dtype), kind="ExternalInput").ap())
    y = nc.dram_tensor("out_y", arrays["in_x"].shape, F32, kind="ExternalOutput").ap()
    build_gat(nc, *args, y)
    r = run_bass_kernel_spmd(nc, [arrays], core_ids=[0])
    return r.results[0]["out_y"]
```

```python
from contextlib import ExitStack

import concourse.bass as bass
from concourse import mybir

ALU = mybir.AluOpType
ACT = mybir.ActivationFunctionType
AX = mybir.AxisListType
F32 = mybir.dt.float32
BF16 = mybir.dt.bfloat16
F16 = mybir.dt.float16
I32 = mybir.dt.int32

P = 128
ALPHA = 0.2
EPS = 1e-5
BIG = 2.0 ** 40
TOP = 2.0 ** 15
LEAST = 2.0 ** -14
SPLIT = 2.0 ** 11
MASKED = -4.5e16


def build_gat(nc, x, adj, W, a, out, s_nodes):
    N, F = x.shape
    FE = F + 1
    FX = F + 2
    FP = 2 * FE
    JB = N // P
    K = 4
    G = JB // K
    WI = P * K
    E = 2
    WU = E * WI
    UC = 2
    CJ = UC * E * P
    RC = 4
    RU = 4
    BU = RC * UC
    QG = JB // (BU * E)
    LEAD = RU - 1
    NR = 4
    RR = JB // NR
    PR = RR // 2
    HP = PR // 2
    assert JB % (BU * E) == 0 and JB % K == 0 and BU % RU == 0 and 2 * F == P and QG == NR and HP % 2 == 0

    ctx = ExitStack()
    with ctx:
        def sb(name, shape, dt=F32):
            return ctx.enter_context(nc.sbuf_tensor(name, shape, dt))

        def sem(name):
            return ctx.enter_context(nc.semaphore(name))

        adj_ring = sb("adj_ring", [P, RC, K, CJ], I32)
        san = sb("san", [P, RC, K, CJ], BF16)
        srow = sb("srow", [P, N])
        Wh = sb("Wh", [P, JB, FX])
        V = sb("V", [P, JB, 3 * FP], F16)
        rings = sb("rings", [P, 2 * RU + BU, WU], BF16)
        mask = rings[:, 0:RU]
        up = rings[:, RU:2 * RU]
        step = rings[:, 2 * RU:2 * RU + BU]
        flat = rings[:, :, :].rearrange("p r w -> p (r w)").bitcast(F32)
        xh = flat[:, 0:JB * F].rearrange("p (r f) -> p r f", f=F)
        sq = san[:, :, :, :].rearrange("p s k j -> p (s k j)").bitcast(F32).rearrange("p (r f) -> p r f", f=F)
        hT = V[:, :, :].rearrange("p j v -> p (j v)")[:, 0:2 * (JB // 2) * P].bitcast(F32)
        ident = sb("ident", [P, P])
        identb = sb("identb", [P, P], BF16)
        ones = sb("ones", [P, P])
        zerob = sb("zerob", [P, 2 * FP], BF16)
        W2 = sb("W2", [P, F])
        WT = sb("WT", [F, P])
        WT2 = sb("WT2", [F, F])
        Wx = sb("Wx", [P, 2 * FX])
        a_sb = sb("a_sb", [F, 2])
        eps = sb("eps", [P, 1])
        stat = sb("stat", [P, 5, JB])
        ext = sb("ext", [P, 3])
        norm2 = sb("norm2", [F, 1])
        ext2 = sb("ext2", [3, 1])
        extd = sb("extd", [3, 3])
        lim = sb("lim", [P, 8])
        uu = sb("uu", [P, 4, JB])
        nt = sb("nt", [P, JB])
        bt = sb("bt", [P, JB])
        yy = sb("yy", [P, JB, 2])
        ab = sb("ab", [P, JB, 2, 2])
        umin = sb("umin", [P, 1])
        flag = sb("flag", [P, 1], I32)
        YT = sb("YT", [P, 2 * RR * FE])
        Y = YT[:, :].rearrange("p (h r f) -> p h r f", h=2, f=FE)
        tree = YT[:, 0:JB // 2 * F].rearrange("p (j f) -> p j f", f=F)
        sT = sb("sT", [JB, P])
        tot = sb("tot", [P, FE])
        acc_sb = sb("acc_sb", [P, K, 2 * FP])
        xg = sb("xg", [P, K, F])
        parts = sb("parts", [P, K, 2, FE])
        sums = sb("sums", [P, K, FE])
        fixd = sb("fixd", [P, K, FE])
        lone = sb("lone", [P, K])
        rden = sb("rden", [P, K])
        hp = sb("hp", [P, K, F])
        neg = sb("neg", [P, K, F])
        res = sb("res", [P, K, F])

        psum = ctx.enter_context(nc.psum_tensor("psum", [P, 8, 512], F32))
        adjT = [psum[:, s, :].bitcast(BF16) for s in range(RU)]
        acc = [psum[:, 4 + k, 0:2 * FP] for k in range(K)]
        total_ps = psum[:, 4, 2 * FP:2 * FP + F]
        hT_ps = [psum[:, 0:2, :], psum[:, 2:4, :]]
        Wh_ps = [psum[:, 4:6, :], psum[:, 6:8, :]]
        half = [psum[:, 0:4, :], psum[:, 4:8, :]]

        s_x = [sem(f"x_loaded_{b}") for b in range(NR)]
        s_w = sem("weights_loaded")
        s_id0 = sem("identity_cleared")
        s_const = sem("constants_made")
        s_sum = sem("sum_ready")
        s_nm = sem("minus_mean_ready")
        s_xc = sem("centred")
        s_sq = sem("squares_ready")
        s_var = sem("variance_ready")
        s_std = sem("deviation_ready")
        s_rstd = sem("reciprocal_ready")
        s_Wcopy = sem("W_copied")
        s_hT = sem("hT_in_psum")
        s_hTc = sem("hT_copied")
        s_Wh = sem("Wh_in_psum")
        s_Whc = sem("Wh_copied")
        s_sTp = sem("s_transposed")
        s_sT = sem("s_transposed_copied")
        s_snode = sem("s_stored")
        s_srow0 = sem("s_of_the_first_group_on_all_partitions")
        s_srow = sem("s_of_the_others_on_all_partitions")
        s_wp = sem("weight_product")
        s_wt = sem("weight_transposed")
        s_wx = sem("weights_extended")
        s_ext = sem("extrema_step")
        s_extp = sem("extrema_product")
        s_lim = sem("limits_ready")
        s_norm = sem("norms_of_W_step")
        s_sq2 = sem("bound_ready")
        s_u = sem("u_written")
        s_us = sem("u_scaled")
        s_small = sem("small_columns_ready")
        s_yy = sem("exponents_ready")
        s_ab = sem("alpha_beta_ready")
        s_umin = sem("umin_ready")
        s_flag = sem("flag_ready")
        s_ab4 = sem("alpha_beta_of_low_parts_ready")
        s_Y = [sem(f"Y_{h}_ready") for h in range(2)]
        s_hi = [sem(f"high_{h}_ready") for h in range(2)]
        s_lo = [sem(f"low_{h}_ready") for h in range(2)]
        s_V = sem("V_negated")
        s_tree = sem("tree_step")

        s_adj = [sem(f"adj_loaded_{s}") for s in range(RC)]
        s_san = [sem(f"chunk_sanitized_{s}") for s in range(RC)]
        s_T = [sem(f"unit_transposed_{u}") for u in range(BU)]
        s_mask = sem("masks_written")
        s_stepA = sem("steps_written_by_ScalarE")
        s_stepV = sem("steps_written_by_VectorE")
        s_up = sem("ups_written")
        s_P = [sem(f"unit_multiplied_{u}") for u in range(RU)]
        s_group = sem("groups_summed")
        s_evac = sem("acc_banks_copied")
        s_accsb = sem("acc_sb_written")
        s_tot = sem("total_copied")
        s_xg = sem("xg_loaded")
        s_fix = sem("pool_step")
        s_rden = sem("denominators_inverted")
        s_neg = sem("negative_part_ready")
        s_exp = sem("exp_ready")
        s_res = sem("result_ready")
        s_out = sem("out_stored")

        ONE = 1
        STEPS = 9

        adj_v = adj.rearrange("(g k p) j -> g p k j", p=P, k=K)
        x_v = x.rearrange("(g k p) f -> g p k f", p=P, k=K)
        out_v = out.rearrange("(g k p) f -> g p k f", p=P, k=K)

        def pair(c):
            return hT[:, c * P:(c + 1) * P]

        with nc.Block() as block:

            @block.sync
            def _(sp):
                xs = x.rearrange("(r p) f -> p r f", p=P)
                with nc.allow_non_contiguous_dma(reason="rows of x, 256 bytes each"):
                    for b in range(NR):
                        sp.dma_start(xh[:, b * RR:(b + 1) * RR, :], xs[:, b * RR:(b + 1) * RR, :])\
                            .then_inc(s_x[b], 16)

                def load(g, q):
                    for s in range(RC):
                        sp.wait_ge(s_san[s], ONE + g * QG + q)
                        sp.dma_start(adj_ring[:, s], adj_v[g, :, :, bass.ds((q * RC + s) * CJ, CJ)])\
                            .then_inc(s_adj[s], 16)

                load(0, 0)
                sp.wait_ge(s_sT, 1)
                sp.dma_start(s_nodes.rearrange("(j p) -> j p", p=P), sT[:, :]).then_inc(s_snode, 16)
                sp.wait_ge(s_snode, 16)
                for c, done in ((slice(0, WI), s_srow0), (slice(WI, N), s_srow)):
                    sp.dma_start(srow[:, c], s_nodes[c].partition_broadcast(P)).then_inc(done, 16)
                with sp.Fori(1, QG) as q:
                    load(0, q)
                with sp.Fori(1, G) as g:
                    with sp.Fori(0, QG) as q:
                        load(g, q)

            @block.gpsimd
            def _(pool):
                pool.sem_inc(s_fix, ONE)
                nc.gpsimd.memset(ident[:, :], 0.0).then_inc(s_id0, 1)
                nc.gpsimd.memset(identb[:, :], 0.0).then_inc(s_id0, 1)
                nc.gpsimd.memset(ones[:, :], 1.0).then_inc(s_const, 1)
                nc.gpsimd.memset(zerob[:, :], 0.0).then_inc(s_const, 1)
                nc.gpsimd.memset(Wx[:, :], 0.0).then_inc(s_const, 1)
                nc.gpsimd.memset(eps[:, :], EPS).then_inc(s_const, 1)
                nc.gpsimd.memset(tot[:, F:FE], float(N)).then_inc(s_const, 1)
                nc.gpsimd.memset(ext[:, 2:3], 0.0).then_inc(s_const, 1)
                pool.wait_ge(s_id0, 2)
                for m in (ident, identb):
                    nc.gpsimd.affine_select(out=m[:, :], in_=m[:, :], compare_op=ALU.not_equal, fill=1.0, base=0,
                                            pattern=[[-1, P]], channel_multiplier=1).then_inc(s_const, 1)
                pool.wait_ge(s_const, 8)
                pool.wait_ge(s_w, 48)
                nc.gpsimd.tensor_copy(Wx[0:F, 0:F], W2[0:F, :]).then_inc(s_Wcopy, 1)
                nc.gpsimd.tensor_copy(Wx[F:P, FX:FX + F], W2[F:P, :]).then_inc(s_Wcopy, 1)
                pool.wait_ge(s_us, 1)
                for r in range(NR):
                    b = slice(r * RR, (r + 1) * RR)
                    for h in range(2):
                        if r == 0 and h == 0:
                            continue
                        if r:
                            pool.wait_ge(s_lo[h], r)
                        nc.gpsimd.tensor_tensor(Y[:, h, :, 0:F], Wh[:, b, 0:F],
                                                uu[:, 2 + h, b].unsqueeze(2).to_broadcast([P, RR, F]), ALU.mult)
                        nc.gpsimd.tensor_copy(Y[:, h, :, F], uu[:, 2 + h, b]).then_inc(s_Y[h], 1)
                for h in range(2):
                    pool.wait_ge(s_lo[h], NR)
                nc.gpsimd.tensor_tensor(tree[:, :, :], Wh[:, 0:JB // 2, 0:F], Wh[:, JB // 2:JB, 0:F],
                                        ALU.add).then_inc(s_tree, 1)
                w, n = JB // 4, 1
                while w >= 1:
                    pool.wait_ge(s_tree, n)
                    nc.gpsimd.tensor_tensor(tree[:, 0:w, :], tree[:, 0:w, :], tree[:, w:2 * w, :],
                                            ALU.add).then_inc(s_tree, 1)
                    w, n = w // 2, n + 1
                pool.wait_ge(s_ab, 1)
                nc.gpsimd.tensor_scalar(ab[:, :, :, 1], ab[:, :, :, 0], 1.0 / SPLIT, None, ALU.mult).then_inc(s_ab4, 1)
                pool.wait_ge(s_ab4, 1)
                for g in range(G):

                    def after(k):
                        pool.wait_ge(s_fix, ONE + g * STEPS + k)

                    pool.dma_start(xg[:, :, :], x_v[g]).then_inc(s_xg, 16)
                    pool.wait_ge(s_accsb, g + 1)
                    acc_v = acc_sb[:, :, :].rearrange("p k (s f) -> p (k s) f", f=FE)
                    nc.gpsimd.tensor_tensor(acc_v, acc_v, ab[:, g * K:(g + 1) * K].rearrange("p k s h -> p (k s h)")
                                            .unsqueeze(2).to_broadcast([P, 4 * K, FE]), ALU.mult).then_inc(s_fix, 1)
                    after(1)
                    acc_h = acc_sb[:, :, :].rearrange("p k (s h f) -> p (k s) h f", h=2, f=FE)
                    nc.gpsimd.tensor_tensor(parts[:, :, :, :].rearrange("p k s f -> p (k s) f"), acc_h[:, :, 0],
                                            acc_h[:, :, 1], ALU.add).then_inc(s_fix, 1)
                    after(2)
                    nc.gpsimd.tensor_tensor(sums[:, :, :], parts[:, :, 0], parts[:, :, 1], ALU.add).then_inc(s_fix, 1)
                    after(3)
                    nc.gpsimd.tensor_scalar(lone[:, :], sums[:, :, F], 0.0, None, ALU.is_equal).then_inc(s_fix, 1)
                    after(4)
                    nc.gpsimd.tensor_tensor(fixd[:, :, :], lone[:, :].unsqueeze(2).to_broadcast([P, K, FE]),
                                            tot[:, :].unsqueeze(1).to_broadcast([P, K, FE]), ALU.mult).then_inc(s_fix, 1)
                    after(5)
                    nc.gpsimd.tensor_tensor(fixd[:, :, :], fixd[:, :, :], sums[:, :, :], ALU.add).then_inc(s_fix, 1)
                    pool.wait_ge(s_rden, g + 1)
                    nc.gpsimd.tensor_tensor(hp[:, :, :], fixd[:, :, 0:F], rden[:, :].unsqueeze(2).to_broadcast([P, K, F]),
                                            ALU.mult).then_inc(s_fix, 1)
                    after(7)
                    nc.gpsimd.tensor_scalar(neg[:, :, :], hp[:, :, :], 0.0, None, ALU.min).then_inc(s_neg, 1)
                    nc.gpsimd.tensor_scalar(hp[:, :, :], hp[:, :, :], 0.0, -1.0, ALU.max, ALU.add).then_inc(s_fix, 1)
                    after(8)
                    pool.wait_ge(s_xg, 16 * g + 16)
                    nc.gpsimd.tensor_tensor(hp[:, :, :], hp[:, :, :], xg[:, :, :], ALU.add).then_inc(s_fix, 1)
                    after(STEPS)
                    pool.wait_ge(s_exp, g + 1)
                    if g:
                        pool.wait_ge(s_out, 16 * g)
                    nc.gpsimd.tensor_tensor(res[:, :, :], hp[:, :, :], neg[:, :, :], ALU.add).then_inc(s_res, 1)
                    pool.wait_ge(s_res, g + 1)
                    pool.dma_start(out_v[g], res[:, :, :]).then_inc(s_out, 16)
                pool.wait_ge(s_out, 16 * G)

            @block.scalar
            def _(act):
                for v in s_san:
                    act.sem_inc(v, ONE)
                act.sem_inc(s_evac, K)
                for h in range(2):
                    act.dma_start(W2[h * F:(h + 1) * F, :], W).then_inc(s_w, 16)
                with nc.allow_non_contiguous_dma(reason="128 numbers"):
                    act.dma_start(a_sb[:, :], a.rearrange("(c f) o -> f (c o)", c=2)).then_inc(s_w, 16)

                def squares(b):
                    r = slice(b * RR, (b + 1) * RR)
                    act.wait_ge(s_xc, b + 1)
                    nc.scalar.activation(sq[:, r], xh[:, r], ACT.Square).then_inc(s_sq, 1)

                def copy_hT(b):
                    act.wait_ge(s_hT, b + 1)
                    nc.scalar.activation(hT[:, b * PR * P:(b + 1) * PR * P].rearrange("p (b w) -> p b w", b=2),
                                         hT_ps[b % 2], ACT.Relu).then_inc(s_hTc, 1)

                def deviation(b):
                    r = slice(b * RR, (b + 1) * RR)
                    act.wait_ge(s_var, b + 1)
                    nc.scalar.activation(stat[:, 3, r], stat[:, 2, r], ACT.Sqrt, bias=eps[:, :],
                                         scale=1.0 / F).then_inc(s_std, 1)

                act.wait_ge(s_wp, 1)
                nc.scalar.activation(WT[:, :], psum[0:F, 7, 0:P], ACT.Copy).then_inc(s_wt, 1)
                squares(0)
                act.wait_ge(s_wp, 2)
                act.wait_ge(s_Wcopy, 2)
                nc.scalar.activation(Wx[0:F, F:FX], psum[0:F, 7, P:P + 2], ACT.Copy).then_inc(s_wx, 1)
                nc.scalar.activation(Wx[F:P, FX + F:2 * FX], psum[F:P, 7, P:P + 2], ACT.Copy).then_inc(s_wx, 1)
                copy_hT(0)
                act.wait_ge(s_const, 8)
                for b in range(1, NR):
                    squares(b)
                    deviation(b - 1)
                    copy_hT(b)
                deviation(NR - 1)
                act.wait_ge(s_norm, 2)
                nc.scalar.activation(ext[0:F, 2:3], norm2[:, :], ACT.Sqrt, scale=float(F)).then_inc(s_sq2, 1)
                act.wait_ge(s_sTp, 1)
                nc.scalar.activation(sT[:, :], psum[0:JB, 1, 0:P], ACT.Copy).then_inc(s_sT, 1)
                act.wait_ge(s_lim, 1)
                t_all = Wh[:, :, F + 1]
                nc.scalar.activation(uu[:, 0], t_all, ACT.Exp, bias=lim[:, 3:4]).then_inc(s_u, 1)
                nc.scalar.activation(uu[:, 1], t_all, ACT.Exp, bias=lim[:, 4:5], scale=ALPHA).then_inc(s_u, 1)
                nc.scalar.activation(bt[:, :], t_all, ACT.Copy, scale=BIG).then_inc(s_small, 1)

                def high_parts(r):
                    b = slice(r * RR, (r + 1) * RR)
                    for h in range(2):
                        act.wait_ge(s_Y[h], r + 1)
                        nc.scalar.activation(V[:, b, 2 * h * FP:2 * h * FP + FE], Y[:, h], ACT.Copy,
                                             scale=1.0 / SPLIT).then_inc(s_hi[h], 1)

                high_parts(0)
                act.wait_ge(s_yy, 2)
                nc.scalar.activation(ab[:, :, :, 0], yy[:, :, :], ACT.Exp).then_inc(s_ab, 1)
                nc.scalar.activation(umin[:, :], lim[:, 1:2], ACT.Exp, bias=lim[:, 3:4], scale=-1.0)\
                    .then_inc(s_umin, 1)

                def prepare(m, g, q):
                    for s in range(RC):
                        u = UC * s
                        act.wait_ge(s_up, m * BU + u + 1)
                        act.wait_ge(s_adj[s], 16 * m + 16)
                        act.wait_ge(s_T[UC * s + UC - 1], ONE + m)
                        nc.scalar.activation(san[:, s], adj_ring[:, s], ACT.Relu).then_inc(s_san[s], 1)
                        for e in range(E):
                            last = nc.scalar.activation(step[:, u, e * WI:(e + 1) * WI], srow[:, bass.ds(g * WI, WI)],
                                                        ACT.Relu, bias=bt[:, bass.ds(q * BU * E + u * E + e, 1)],
                                                        scale=BIG)
                        last.then_inc(s_stepA, 1)

                def copy_sums(g):
                    act.wait_ge(s_group, g + 1)
                    act.wait_ge(s_fix, ONE + g * STEPS)
                    nc.scalar.activation(tot[:, 0:F], total_ps, ACT.Copy).then_inc(s_tot, 1)
                    for k in range(K):
                        nc.scalar.activation(acc_sb[:, k], acc[k], ACT.Copy).then_inc(s_evac, 1)
                    act.wait_ge(s_evac, K + (g + 1) * K)
                    act.wait_ge(s_tot, g + 1)
                    act.sem_inc(s_accsb, 1)

                def exp_part(g):
                    act.wait_ge(s_neg, g + 1)
                    nc.scalar.activation(neg[:, :, :], neg[:, :, :], ACT.Exp).then_inc(s_exp, 1)

                act.wait_ge(s_var, NR)
                act.wait_ge(s_small, 1)
                act.wait_ge(s_hT, NR)
                act.wait_ge(s_srow0, 16)
                for q in range(QG):
                    prepare(q, 0, q)
                    if q + 1 < NR:
                        high_parts(q + 1)
                act.wait_ge(s_srow, 16)
                with act.Fori(0, G - 1) as g:
                    prepare((g + 1) * QG, g + 1, 0)
                    copy_sums(g)
                    prepare((g + 1) * QG + 1, g + 1, 1)
                    prepare((g + 1) * QG + 2, g + 1, 2)
                    exp_part(g)
                    prepare((g + 1) * QG + 3, g + 1, 3)
                copy_sums(G - 1)
                exp_part(G - 1)

            @block.vector
            def _(dve):
                dve.sem_inc(s_mask, RU)
                dve.sem_inc(s_up, BU)

                def centre(b):
                    r = slice(b * RR, (b + 1) * RR)
                    dve.wait_ge(s_x[b], 16)
                    nc.vector.reduce_sum(stat[:, 0, r], xh[:, r], axis=AX.X).then_inc(s_sum, 1)
                    dve.wait_ge(s_sum, b + 1)
                    nc.vector.tensor_scalar(stat[:, 1, r], stat[:, 0, r], -1.0 / F, None, ALU.mult).then_inc(s_nm, 1)
                    dve.wait_ge(s_nm, b + 1)
                    nc.vector.tensor_tensor(xh[:, r], xh[:, r], stat[:, 1, r].unsqueeze(2).to_broadcast([P, RR, F]),
                                            ALU.add).then_inc(s_xc, 1)

                def variance(b):
                    r = slice(b * RR, (b + 1) * RR)
                    dve.wait_ge(s_sq, b + 1)
                    nc.vector.reduce_sum(stat[:, 2, r], sq[:, r], axis=AX.X).then_inc(s_var, 1)

                def copy_Wh(b):
                    r = slice(b * RR, (b + 1) * RR)
                    dve.wait_ge(s_std, b + 1)
                    nc.vector.reciprocal(stat[:, 4, r], stat[:, 3, r]).then_inc(s_rstd, 1)
                    dve.wait_ge(s_rstd, b + 1)
                    for i in range(2):
                        r = slice(b * RR + i * 2 * HP, b * RR + (i + 1) * 2 * HP)
                        dve.wait_ge(s_Wh, 2 * b + i + 1)
                        nc.vector.tensor_tensor(Wh[:, r, :].rearrange("p (b j) f -> p b j f", b=2),
                                                Wh_ps[i][:, :, 0:HP * FX].rearrange("p b (j f) -> p b j f", f=FX),
                                                stat[:, 4, r].rearrange("p (b j) -> p b j", b=2).unsqueeze(3)
                                                .to_broadcast([P, 2, HP, FX]), ALU.mult).then_inc(s_Whc, 1)

                centre(0)
                centre(1)
                variance(0)
                centre(2)
                variance(1)
                copy_Wh(0)
                centre(3)
                variance(2)
                copy_Wh(1)
                variance(3)
                dve.wait_ge(s_wt, 1)
                nc.vector.tensor_tensor(WT2[:, :], WT[:, 0:F], WT[:, 0:F], ALU.mult).then_inc(s_norm, 1)
                dve.wait_ge(s_norm, 1)
                nc.vector.reduce_sum(norm2[:, :], WT2[:, :], axis=AX.X).then_inc(s_norm, 1)
                copy_Wh(2)
                copy_Wh(3)
                dve.wait_ge(s_Whc, 2 * NR)
                t_all = Wh[:, :, F + 1]
                nc.vector.tensor_reduce(ext[:, 0:1], t_all, AX.X, ALU.max).then_inc(s_ext, 1)
                nc.vector.tensor_reduce(ext[:, 1:2], t_all, AX.X, ALU.min).then_inc(s_ext, 1)
                dve.wait_ge(s_ext, 2)
                nc.vector.tensor_scalar(ext[:, 1:2], ext[:, 1:2], -1.0, None, ALU.mult).then_inc(s_ext, 1)
                dve.wait_ge(s_extp, 1)
                nc.vector.tensor_reduce(ext2[:, 0:1], psum[0:3, 0, 0:P], AX.X, ALU.max).then_inc(s_ext, 1)
                dve.wait_ge(s_ext, 4)
                nc.vector.tensor_scalar(extd[:, :], ident[0:3, 0:3], ext2[:, 0:1], None, ALU.mult).then_inc(s_ext, 1)
                dve.wait_ge(s_extp, 2)
                nc.vector.tensor_copy(lim[:, 0:3], psum[:, 0, P:P + 3]).then_inc(s_ext, 1)
                dve.wait_ge(s_ext, 6)
                nc.vector.tensor_scalar(lim[:, 3:4], lim[:, 0:1], -1.0, None, ALU.mult)
                nc.vector.tensor_scalar(lim[:, 4:5], lim[:, 0:1], -ALPHA, None, ALU.mult)
                nc.vector.tensor_scalar(lim[:, 5:6], lim[:, 2:3], 1.0, 1.0 / (TOP * SPLIT), ALU.max, ALU.mult).then_inc(s_lim, 1)
                dve.wait_ge(s_lim, 1)
                nc.vector.reciprocal(lim[:, 6:7], lim[:, 5:6]).then_inc(s_lim, 1)
                dve.wait_ge(s_u, 2)
                dve.wait_ge(s_lim, 2)
                nc.vector.tensor_scalar(uu[:, 2:4], uu[:, 0:2], lim[:, 6:7], None, ALU.mult).then_inc(s_us, 1)
                dve.wait_ge(s_us, 1)
                r = slice(0, RR)
                nc.vector.tensor_tensor(Y[:, 0, :, 0:F], Wh[:, r, 0:F],
                                        uu[:, 2, r].unsqueeze(2).to_broadcast([P, RR, F]), ALU.mult)
                nc.vector.tensor_copy(Y[:, 0, :, F], uu[:, 2, r]).then_inc(s_Y[0], 1)

                def low_parts(r):
                    b = slice(r * RR, (r + 1) * RR)
                    for h in range(2):
                        o = 2 * h * FP
                        dve.wait_ge(s_hi[h], r + 1)
                        nc.vector.scalar_tensor_tensor(out=V[:, b, o + FE:o + FP], in0=V[:, b, o:o + FE],
                                                       scalar=-SPLIT, in1=Y[:, h], op0=ALU.mult, op1=ALU.add)\
                            .then_inc(s_lo[h], 1)
                    dve.wait_ge(s_lo[1], r + 1)
                    nc.vector.tensor_scalar(V[:, b, FP:2 * FP], V[:, b, 2 * FP:3 * FP], -1.0, None,
                                            ALU.mult).then_inc(s_V, 1)

                s_all = Wh[:, :, F]
                nc.vector.tensor_scalar(yy[:, :, 0], s_all, lim[:, 0:1], 1 - ALPHA, ALU.add, ALU.mult).then_inc(s_yy, 1)
                dve.wait_ge(s_yy, 1)
                nc.vector.tensor_scalar(yy[:, :, 1], yy[:, :, 0], -1.0, 0.0, ALU.mult, ALU.min).then_inc(s_ext, 1)
                dve.wait_ge(s_ext, 7)
                nc.vector.tensor_scalar(yy[:, :, 0], yy[:, :, 0], 0.0, None, ALU.min).then_inc(s_yy, 1)
                nc.vector.tensor_scalar(nt[:, :], Wh[:, :, F + 1], -1.0, None, ALU.mult).then_inc(s_ext, 1)
                low_parts(0)
                dve.wait_ge(s_umin, 1)
                nc.vector.tensor_scalar(flag[:, :], umin[:, :], lim[:, 6:7], LEAST * SPLIT, ALU.mult, ALU.is_lt)\
                    .then_inc(s_flag, 1)
                dve.wait_ge(s_srow0, 16)
                dve.wait_ge(s_ext, 8)
                dve.wait_ge(s_hT, NR)

                def take_up(m, u):
                    dve.wait_ge(s_mask, RU + m * BU + u + 1)
                    dve.wait_ge(s_stepV if u % 2 else s_stepA, m * (BU // 2) + u // 2 + 1)
                    nc.vector.tensor_tensor(up[:, u % RU], mask[:, u % RU], step[:, u], ALU.min).then_inc(s_up, 1)

                def mask_unit(m, g, q, u):
                    dve.wait_ge(s_T[u], ONE + m + 1)
                    dve.wait_ge(s_P[u % RU], ONE + m * (BU // RU) + u // RU)
                    nc.vector.tensor_scalar(mask[:, u % RU], adjT[u % RU], 0.0, None, ALU.is_gt).then_inc(s_mask, 1)
                    if u % 2:
                        dve.wait_ge(s_up, m * BU + u + 1)
                        for e in range(E):
                            last = nc.vector.tensor_scalar(step[:, u, e * WI:(e + 1) * WI],
                                                           srow[:, bass.ds(g * WI, WI)],
                                                           nt[:, bass.ds(q * BU * E + u * E + e, 1)], None,
                                                           ALU.is_ge)
                        last.then_inc(s_stepV, 1)
                    if u:
                        take_up(m, u - 1)

                def masks(g, first, bodies):
                    with dve.Fori(first, first + bodies) as q:
                        for u in range(BU):
                            mask_unit(g * QG + q, g, q, u)
                        take_up(g * QG + q, BU - 1)

                def invert(g):
                    dve.wait_ge(s_fix, ONE + g * STEPS + 6)
                    nc.vector.reciprocal(rden[:, :], fixd[:, :, F]).then_inc(s_rden, 1)

                for q in range(QG):
                    for u in range(BU):
                        mask_unit(q, 0, q, u)
                        if u == BU // 2 and q + 1 < NR:
                            low_parts(q + 1)
                    take_up(q, BU - 1)
                dve.wait_ge(s_srow, 16)
                with dve.Fori(0, G - 1) as g:
                    masks(g + 1, 0, 2)
                    invert(g)
                    masks(g + 1, 2, QG - 2)
                invert(G - 1)

            @block.tensor
            def _(pe):
                for v in s_T + s_P:
                    pe.sem_inc(v, ONE)
                pe.wait_ge(s_w, 48)
                pe.wait_ge(s_const, 8)
                nc.tensor.transpose(psum[0:F, 7, 0:P], W2[:, :], ident[:, :]).then_inc(s_wp, 1)
                pe.wait_ge(s_wt, 1)
                nc.tensor.matmul(psum[:, 7, P:P + 2], WT[:, :], a_sb[:, :], start=True, stop=True).then_inc(s_wp, 1)

                def transpose_round(b):
                    pe.wait_ge(s_xc, b + 1)
                    if b >= 2:
                        pe.wait_ge(s_hTc, b - 1)
                    for c in range(PR):
                        r = 2 * (b * PR + c)
                        last = nc.tensor.transpose(hT_ps[b % 2][:, c // 4, (c % 4) * P:(c % 4 + 1) * P],
                                                   xh[:, r:r + 2, :].rearrange("p r f -> p (r f)"), ident[:, :])
                    last.then_inc(s_hT, 1)

                def Wh_half_rounds(b):
                    pe.wait_ge(s_hTc, b + 1)
                    for i in range(2):
                        if b:
                            pe.wait_ge(s_Whc, 2 * b + i - 1)
                        for c in range(HP):
                            last = nc.tensor.matmul(Wh_ps[i][:, c // (HP // 2), (c % (HP // 2)) * 2 * FX:
                                                             (c % (HP // 2) + 1) * 2 * FX],
                                                    pair(b * PR + i * HP + c), Wx[:, :], start=True, stop=True)
                        last.then_inc(s_Wh, 1)

                transpose_round(0)
                pe.wait_ge(s_wx, 2)
                for b in range(NR):
                    if b + 1 < NR:
                        transpose_round(b + 1)
                    Wh_half_rounds(b)
                pe.wait_ge(s_Whc, 2 * NR)
                nc.tensor.transpose(psum[0:JB, 1, 0:P], Wh[:, :, F], ident[:, :]).then_inc(s_sTp, 1)
                pe.wait_ge(s_ext, 3)
                pe.wait_ge(s_sq2, 1)
                nc.tensor.transpose(psum[0:3, 0, 0:P], ext[:, :], ident[:, :]).then_inc(s_extp, 1)
                pe.wait_ge(s_ext, 5)
                nc.tensor.matmul(psum[:, 0, P:P + 3], ones[0:3, :], extd[:, :], start=True, stop=True).then_inc(s_extp, 1)
                def transpose_unit(m, u):
                    if u % UC == 0:
                        pe.wait_ge(s_san[u // UC], ONE + m + 1)
                    pe.wait_ge(s_mask, m * BU + u + 1)
                    for e in range(E):
                        for k in range(K):
                            c = (u % UC) * E + e
                            b = e * K + k
                            last = nc.tensor.transpose(adjT[u % RU][:, b * P:(b + 1) * P],
                                                       san[:, u // UC, k, c * P:(c + 1) * P], identb[:, :])
                    last.then_inc(s_T[u], 1)

                def multiply_unit(m, u, q):
                    if u == 0:
                        pe.wait_ge(s_V, q + 1)
                    pe.wait_ge(s_up, BU + m * BU + u + 1)
                    for e in range(E):
                        v = V[:, bass.ds(q * BU * E + u * E + e, 1), :].rearrange("p o v -> p (o v)")
                        for k in range(K):
                            b = e * K + k
                            nc.tensor.matmul(acc[k][:, FP:2 * FP], mask[:, u % RU, b * P:(b + 1) * P],
                                             v[:, 2 * FP:3 * FP], start=False, stop=False, skip_group_check=True)
                            last = nc.tensor.matmul(acc[k], up[:, u % RU, b * P:(b + 1) * P], v[:, 0:2 * FP],
                                                    start=False, stop=False, skip_group_check=True)
                    last.then_inc(s_P[u % RU], 1)

                def body(m, q, last=False):
                    for u in range(BU):
                        if u + LEAD < BU:
                            transpose_unit(m, u + LEAD)
                        elif not last:
                            transpose_unit(m + 1, u + LEAD - BU)
                        multiply_unit(m, u, q)

                def open_group(g):
                    for k in range(K):
                        pe.wait_ge(s_evac, g * K + k + 1)
                        nc.tensor.matmul(acc[k], identb[:, :], zerob[:, :], start=True, stop=False,
                                         skip_group_check=True)

                def close_group():
                    pe.wait_ge(s_tree, 6)
                    nc.tensor.matmul(total_ps, ones[:, :], tree[:, 0, :], start=False, stop=True,
                                     skip_group_check=True).then_inc(s_group, 1)

                pe.wait_ge(s_lim, 1)
                pe.wait_ge(s_sT, 1)
                for u in range(LEAD):
                    transpose_unit(0, u)
                with pe.Fori(0, G - 1) as g:
                    open_group(g)
                    with pe.Fori(0, QG) as q:
                        body(g * QG + q, q)
                    close_group()
                open_group(G - 1)
                with pe.Fori(0, QG - 1) as q:
                    body((G - 1) * QG + q, q)
                body(G * QG - 1, QG - 1, last=True)
                close_group()

        A = adj_ring[:, :, :, :].rearrange("p s k j -> p (s k j)")
        score = flat
        trow = srow
        whole = V[:, :, :].rearrange("p j v -> p (j v)").bitcast(F32)
        Wh1 = whole[:, 0:JB * FE].rearrange("p (j f) -> p j f", f=FE)
        probT = whole[:, JB * FE:JB * FE + N]
        xt, hpt, negt, rest = xg[:, 0], hp[:, 0], neg[:, 0], res[:, 0]
        rdent, rowmax = rden[:, 0:1], lone[:, 0:1]
        acc1 = psum[:, 0, 0:FE]
        Q = N // NR
        DSTEPS = 9

        def trow_round(r):
            return trow[:, r * Q:(r + 1) * Q].rearrange("q (b w) -> q b w", b=4), half[r % 2]

        def probT_round(r):
            return probT[:, r * Q:(r + 1) * Q].rearrange("q (b w) -> q b w", b=4), half[r % 2]

        g_adj = sem("general_adj_loaded")
        g_x = sem("general_x_loaded")
        g_read = sem("general_adj_read")
        g_dve = sem("general_step_of_VectorE")
        g_round = sem("general_round_in_psum")
        g_even = sem("general_even_round_copied")
        g_odd = sem("general_odd_round_copied")
        g_prob = sem("general_probabilities_ready")
        g_acc = sem("general_rows_summed")
        g_fin = sem("general_last_steps")
        g_neg = sem("general_negative_part_exp")
        g_res = sem("general_result_ready")
        g_out = sem("general_out_stored")

        def needed(engine):
            return engine.value_load(flag[0:1, 0:1], min_val=0, max_val=1) != 0

        with nc.Block() as general:

            @general.sync
            def _(sp):
                with sp.If(needed(sp)):
                    sp.sem_inc(g_out, ONE)
                    with sp.Fori(0, JB) as i:
                        sp.wait_ge(g_read, ONE + i)
                        sp.dma_start(A, adj[bass.ds(i * P, P), :]).then_inc(g_adj, 16)
                        sp.wait_ge(g_res, ONE + i)
                        sp.dma_start(xt, x[bass.ds(i * P, P), :]).then_inc(g_x, 16)

            @general.scalar
            def _(act):
                with act.If(needed(act)):
                    for r in (1, 3):
                        act.wait_ge(g_round, r + 1)
                        nc.scalar.activation(*trow_round(r), ACT.Copy).then_inc(g_odd, 1)
                    with act.Fori(0, JB) as i:
                        act.wait_ge(g_dve, i * DSTEPS + 6)
                        for r in range(NR):
                            nc.scalar.activation(score[:, r * Q:(r + 1) * Q], score[:, r * Q:(r + 1) * Q], ACT.Exp,
                                                 bias=rowmax).then_inc(g_prob, 1)
                        for r in (1, 3):
                            act.wait_ge(g_round, NR + i * NR + r + 1)
                            nc.scalar.activation(*probT_round(r), ACT.Copy).then_inc(g_odd, 1)
                        act.wait_ge(g_dve, i * DSTEPS + 9)
                        nc.scalar.activation(negt, negt, ACT.Exp).then_inc(g_neg, 1)
                        act.wait_ge(g_res, ONE + i + 1)
                        act.dma_start(out[bass.ds(i * P, P), :], rest).then_inc(g_out, 16)
                    act.wait_ge(g_out, ONE + 16 * JB)

            @general.vector
            def _(dve):
                with dve.If(needed(dve)):
                    dve.sem_inc(g_read, ONE)
                    dve.sem_inc(g_res, ONE)
                    for r in (0, 2):
                        dve.wait_ge(g_round, r + 1)
                        nc.vector.tensor_copy(*trow_round(r)).then_inc(g_even, 1)
                    nc.vector.tensor_copy(Wh1[:, :, 0:F], Wh[:, :, 0:F]).then_inc(g_even, 1)
                    nc.vector.memset(Wh1[:, :, F:FE], 1.0).then_inc(g_even, 1)
                    dve.wait_ge(g_even, 2)
                    dve.wait_ge(g_odd, 2)
                    with dve.Fori(0, JB) as i:

                        def after(k):
                            dve.wait_ge(g_dve, i * DSTEPS + k)

                        dve.wait_ge(g_adj, 16 * i + 16)
                        nc.vector.tensor_scalar(score, A, 0.0, None, ALU.is_gt).then_inc(g_read, 1)
                        dve.wait_ge(g_read, ONE + i + 1)
                        nc.vector.tensor_scalar(score, score, -1.0, -MASKED, ALU.add, ALU.mult).then_inc(g_dve, 1)
                        after(1)
                        nc.vector.tensor_tensor(score, score, trow[:, :], ALU.add).then_inc(g_dve, 1)
                        after(2)
                        nc.vector.tensor_scalar(score, score, Wh[:, bass.ds(i, 1), F], None, ALU.add)\
                            .then_inc(g_dve, 1)
                        after(3)
                        nc.vector.scalar_tensor_tensor(out=score, in0=score, scalar=ALPHA, in1=score, op0=ALU.mult,
                                                       op1=ALU.max).then_inc(g_dve, 1)
                        after(4)
                        nc.vector.tensor_reduce(rowmax, score, AX.X, ALU.max).then_inc(g_dve, 1)
                        after(5)
                        nc.vector.tensor_scalar(rowmax, rowmax, -1.0, None, ALU.mult).then_inc(g_dve, 1)
                        for r in (0, 2):
                            dve.wait_ge(g_round, NR + i * NR + r + 1)
                            nc.vector.tensor_copy(*probT_round(r)).then_inc(g_even, 1)
                        dve.wait_ge(g_acc, i + 1)
                        nc.vector.reciprocal(rdent, acc1[:, F:FE]).then_inc(g_dve, 1)
                        after(7)
                        nc.vector.tensor_scalar(hpt, acc1[:, 0:F], rdent, None, ALU.mult).then_inc(g_dve, 1)
                        after(8)
                        nc.vector.tensor_scalar(negt, hpt, 0.0, None, ALU.min).then_inc(g_dve, 1)
                        dve.wait_ge(g_neg, i + 1)
                        nc.vector.tensor_scalar(hpt, hpt, 0.0, -1.0, ALU.max, ALU.add).then_inc(g_fin, 1)
                        dve.wait_ge(g_fin, 2 * i + 1)
                        nc.vector.tensor_tensor(hpt, hpt, negt, ALU.add).then_inc(g_fin, 1)
                        dve.wait_ge(g_fin, 2 * i + 2)
                        dve.wait_ge(g_x, 16 * i + 16)
                        dve.wait_ge(g_out, ONE + 16 * i)
                        nc.vector.tensor_tensor(rest, hpt, xt, ALU.add).then_inc(g_res, 1)

            @general.tensor
            def _(pe):
                with pe.If(needed(pe)):
                    for r in range(NR):
                        if r >= 2:
                            pe.wait_ge(g_even if r % 2 == 0 else g_odd, r // 2)
                        for j in range(RR):
                            jb = r * RR + j
                            last = nc.tensor.transpose(half[r % 2][:, j // 4, (j % 4) * P:(j % 4 + 1) * P],
                                                       Wh[:, jb, F + 1:FX].to_broadcast([P, P]), ident[:, :])
                        last.then_inc(g_round, 1)
                    pe.wait_ge(g_even, 4)
                    pe.wait_ge(g_odd, 2)
                    with pe.Fori(0, JB) as i:
                        pe.wait_ge(g_res, ONE + i)
                        for r in range(NR):
                            pe.wait_ge(g_prob, i * NR + r + 1)
                            if r >= 2:
                                pe.wait_ge(g_even if r % 2 == 0 else g_odd, (4 if r % 2 == 0 else 2) + 2 * i + r // 2)
                            for j in range(RR):
                                jb = r * RR + j
                                last = nc.tensor.transpose(half[r % 2][:, j // 4, (j % 4) * P:(j % 4 + 1) * P],
                                                           score[:, jb * P:(jb + 1) * P], ident[:, :])
                            last.then_inc(g_round, 1)
                        pe.wait_ge(g_even, 4 + 2 * i + 2)
                        pe.wait_ge(g_odd, 2 + 2 * i + 2)
                        for jb in range(JB):
                            last = nc.tensor.matmul(acc1, probT[:, jb * P:(jb + 1) * P], Wh1[:, jb, :],
                                                    start=jb == 0, stop=jb == JB - 1)
                        last.then_inc(g_acc, 1)


_INS = ["x", "adj", "L0_gnn_W", "L0_gnn_a"]


def kernel(**inputs):
    import numpy as np
    import concourse.bacc as bacc
    from concourse.bass_utils import run_bass_kernel_spmd

    nc = bacc.Bacc("TRN2", target_bir_lowering=False, num_devices=1)
    arrays, args = {}, []
    for name in _INS:
        v = np.ascontiguousarray(inputs[name])
        arrays[f"in_{name}"] = v
        args.append(nc.dram_tensor(f"in_{name}", v.shape, mybir.dt.from_np(v.dtype), kind="ExternalInput").ap())
    y = nc.dram_tensor("out_y", arrays["in_x"].shape, F32, kind="ExternalOutput").ap()
    s_nodes = nc.dram_tensor("s_nodes", [arrays["in_x"].shape[0]], F32, kind="Internal").ap()
    build_gat(nc, *args, y, s_nodes)
    r = run_bass_kernel_spmd(nc, [arrays], core_ids=[0])
    return r.results[0]["out_y"]
```

```python
from contextlib import ExitStack

import concourse.bass as bass
from concourse import mybir

ALU = mybir.AluOpType
ACT = mybir.ActivationFunctionType
AX = mybir.AxisListType
F32 = mybir.dt.float32
BF16 = mybir.dt.bfloat16
F16 = mybir.dt.float16
I32 = mybir.dt.int32

P = 128
ALPHA = 0.2
EPS = 1e-5
BIG = 2.0 ** 40
TOP = 2.0 ** 15
LEAST = 2.0 ** -14
SPLIT = 2.0 ** 11
MASKED = -4.5e16


def build_gat(nc, x, adj, W, a, out, s_nodes):
    N, F = x.shape
    FE = F + 1
    FX = F + 2
    FP = 2 * FE
    JB = N // P
    K = 8
    G = JB // K
    WI = P * K
    KE = K // 2
    WU = WI
    UC = 2
    CJ = UC * P
    RC = 4
    TB = 2
    RU = 4
    BU = RC * UC
    QG = JB // BU
    AS = (0, 2, 4, 6, 7)
    VS = [u for u in range(BU) if u not in AS]
    DN = (1, 5)
    NS = 3
    NA = (2 * K + NS - 1) // NS
    LEAD = RU - 1
    NR = 4
    RR = JB // NR
    PR = RR // 2
    HP = PR // 2
    assert JB % BU == 0 and JB % K == 0 and BU % RU == 0 and 2 * F == P and HP % 2 == 0 and TB + NA == 8

    ctx = ExitStack()
    with ctx:
        def sb(name, shape, dt=F32):
            return ctx.enter_context(nc.sbuf_tensor(name, shape, dt))

        def sem(name):
            return ctx.enter_context(nc.semaphore(name))

        adj_ring = sb("adj_ring", [P, RC, K, CJ], I32)
        san = sb("san", [P, RC, K, CJ], BF16)
        srow = sb("srow", [P, N])
        Wh = sb("Wh", [P, JB, FX])
        V = sb("V", [P, JB, 3 * FP], F16)
        rings = sb("rings", [P, 2 * RU + BU, WU], BF16)
        mask = rings[:, 0:RU]
        up = rings[:, RU:2 * RU]
        step = rings[:, 2 * RU:2 * RU + BU]
        flat = rings[:, :, :].rearrange("p r w -> p (r w)").bitcast(F32)
        xh = flat[:, 0:JB * F].rearrange("p (r f) -> p r f", f=F)
        sq = san[:, :, :, :].rearrange("p s k j -> p (s k j)").bitcast(F32).rearrange("p (r f) -> p r f", f=F)
        hT = V[:, :, :].rearrange("p j v -> p (j v)")[:, 0:2 * (JB // 2) * P].bitcast(F32)
        ident = sb("ident", [P, P])
        identb = sb("identb", [P, P], BF16)
        ones = sb("ones", [P, P])
        zerob = sb("zerob", [P, NS * FP], BF16)
        W2 = sb("W2", [P, F])
        WT = sb("WT", [F, P])
        WT2 = sb("WT2", [F, F])
        Wx = sb("Wx", [P, 2 * FX])
        a_sb = sb("a_sb", [F, 2])
        eps = sb("eps", [P, 1])
        stat = sb("stat", [P, 5, JB])
        ext = sb("ext", [P, 3])
        norm2 = sb("norm2", [F, 1])
        ext2 = sb("ext2", [3, 1])
        extd = sb("extd", [3, 3])
        lim = sb("lim", [P, 8])
        uu = sb("uu", [P, 4, JB])
        nt = sb("nt", [P, JB])
        bt = sb("bt", [P, JB])
        yy = sb("yy", [P, JB, 2])
        ab = sb("ab", [P, JB, 2, 2])
        umin = sb("umin", [P, 1])
        flag = sb("flag", [P, 1], I32)
        pool_mem = sb("pool_mem", [P, 4 * BU * FE])
        Y = pool_mem[:, :].rearrange("p (b h r f) -> p b h r f", b=2, h=2, f=FE)
        tree = pool_mem[:, 0:JB // 2 * F].rearrange("p (j f) -> p j f", f=F)
        acc_sb = pool_mem[:, 0:2 * K * FP]
        wh_sum = sb("wh_sum", [P, F])
        sT = sb("sT", [JB, P])
        tot = sb("tot", [P, FE])
        xg = sb("xg", [P, KE, F])
        parts = sb("parts", [P, KE, 2, FE])
        sums = sb("sums", [P, KE, FE])
        fixd = sb("fixd", [P, KE, FE])
        lone = sb("lone", [P, KE])
        rden = sb("rden", [P, KE])
        hp = sb("hp", [P, KE, F])
        neg = sb("neg", [P, KE, F])
        res = sb("res", [P, KE, F])

        psum = ctx.enter_context(nc.psum_tensor("psum", [P, 8, 512], F32))
        adjT = [psum[:, s, :].bitcast(BF16) for s in range(TB)]
        sum_bank = [psum[:, TB + b, :] for b in range(NA)]
        total_ps = sum_bank[NA - 1][:, FP:FP + F]
        spare = adj_ring[:, :, :, :].rearrange("p s k j -> p (s k j)").bitcast(F32)
        hT_ps = [psum[:, 0:2, :], psum[:, 2:4, :]]
        Wh_ps = [psum[:, 4:6, :], psum[:, 6:8, :]]
        half = [psum[:, 0:4, :], psum[:, 4:8, :]]

        s_x = [sem(f"x_loaded_{b}") for b in range(NR)]
        s_w = sem("weights_loaded")
        s_id0 = sem("identity_cleared")
        s_const = sem("constants_made")
        s_sum = sem("sum_ready")
        s_nm = sem("minus_mean_ready")
        s_xc = sem("centred")
        s_sq = sem("squares_ready")
        s_var = sem("variance_ready")
        s_std = sem("deviation_ready")
        s_rstd = sem("reciprocal_ready")
        s_Wcopy = sem("W_copied")
        s_hT = sem("hT_in_psum")
        s_hTc = sem("hT_copied")
        s_Wh = sem("Wh_in_psum")
        s_Whc = sem("Wh_copied")
        s_sTp = sem("s_transposed")
        s_sT = sem("s_transposed_copied")
        s_snode = sem("s_stored")
        s_srow0 = sem("s_of_the_first_group_on_all_partitions")
        s_srow = sem("s_of_the_others_on_all_partitions")
        s_wp = sem("weight_product")
        s_wt = sem("weight_transposed")
        s_wx = sem("weights_extended")
        s_ext = sem("extrema_step")
        s_extp = sem("extrema_product")
        s_lim = sem("limits_ready")
        s_norm = sem("norms_of_W_step")
        s_sq2 = sem("bound_ready")
        s_u = sem("u_written")
        s_us = sem("u_scaled")
        s_small = sem("small_columns_ready")
        s_yy = sem("exponents_ready")
        s_ab = sem("alpha_beta_ready")
        s_umin = sem("umin_ready")
        s_flag = sem("flag_ready")
        s_ab4 = sem("alpha_beta_of_low_parts_ready")
        s_Y0 = sem("Y_0_of_the_first_round_ready")
        s_Y = [sem(f"Y_{h}_ready") for h in range(2)]
        s_hi = [sem(f"high_{h}_ready") for h in range(2)]
        s_lo = [sem(f"low_{h}_ready") for h in range(2)]
        s_V = sem("V_negated")
        s_tree = sem("tree_step")

        s_adj = [sem(f"adj_loaded_{s}") for s in range(RC)]
        s_san = [sem(f"chunk_sanitized_{s}") for s in range(RC)]
        s_T = [sem(f"unit_transposed_{u}") for u in range(BU)]
        s_mask = sem("masks_written")
        s_stepA = sem("steps_written_by_ScalarE")
        s_stepV = sem("steps_written_by_VectorE")
        s_up = sem("ups_written")
        s_P = [sem(f"unit_multiplied_{u}") for u in range(RU)]
        s_group = sem("groups_summed")
        s_evac = [sem(f"sum_bank_{b}_copied") for b in range(NA)] + [sem("total_copied")]
        s_down = sem("downs_written")
        s_xl = sem("x_of_last_group_loaded")
        s_tail = sem("step_of_last_group")
        s_lneg = sem("exp_of_last_group_ready")
        s_xg = sem("xg_loaded")
        s_fix = sem("pool_step")
        s_rden = sem("denominators_inverted")
        s_neg = sem("negative_part_ready")
        s_exp = sem("exp_ready")
        s_res = sem("result_ready")
        s_out = sem("out_stored")

        ONE = 1
        STEPS = 9

        adj_v = adj.rearrange("(g k p) j -> g p k j", p=P, k=K)
        x_v = x.rearrange("(c k p) f -> c p k f", p=P, k=KE)
        out_v = out.rearrange("(c k p) f -> c p k f", p=P, k=KE)

        TSTEPS = 11
        cuts = [2 * K * FE, K * FE, K * FE, K * F, K * F, K * F, K * F]
        at = [sum(cuts[:i]) for i in range(len(cuts) + 1)]
        lparts = spare[:, at[0]:at[1]].rearrange("p (k f) -> p k f", f=FE)
        lsum, lfix = [spare[:, at[i]:at[i + 1]].rearrange("p (k f) -> p k f", f=FE) for i in (1, 2)]
        lx, lhp, lneg, lres = [spare[:, at[i]:at[i + 1]].rearrange("p (k f) -> p k f", f=F) for i in (3, 4, 5, 6)]
        llone, lrden = spare[:, at[7]:at[7] + K], spare[:, at[7] + K:at[7] + 2 * K]

        def pair(c):
            return hT[:, c * P:(c + 1) * P]

        with nc.Block() as block:

            @block.sync
            def _(sp):
                xs = x.rearrange("(r p) f -> p r f", p=P)
                with nc.allow_non_contiguous_dma(reason="rows of x, 256 bytes each"):
                    for b in range(NR):
                        sp.dma_start(xh[:, b * RR:(b + 1) * RR, :], xs[:, b * RR:(b + 1) * RR, :])\
                            .then_inc(s_x[b], 16)

                def load(g, q):
                    for s in range(RC):
                        sp.wait_ge(s_san[s], ONE + g * QG + q)
                        sp.dma_start(adj_ring[:, s], adj_v[g, :, :, bass.ds((q * RC + s) * CJ, CJ)])\
                            .then_inc(s_adj[s], 16)

                load(0, 0)
                sp.wait_ge(s_sT, 1)
                sp.dma_start(s_nodes.rearrange("(j p) -> j p", p=P), sT[:, :]).then_inc(s_snode, 16)
                sp.wait_ge(s_snode, 16)
                for c, done in ((slice(0, WI), s_srow0), (slice(WI, N), s_srow)):
                    sp.dma_start(srow[:, c], s_nodes[c].partition_broadcast(P)).then_inc(done, 16)
                with sp.Fori(1, QG) as q:
                    load(0, q)
                with sp.Fori(1, G) as g:
                    with sp.Fori(0, QG) as q:
                        load(g, q)
                for v in s_san:
                    sp.wait_ge(v, ONE + G * QG)
                last = slice((G - 1) * WI, N)
                sp.dma_start(lx, x[last].rearrange("(k p) f -> p k f", p=P)).then_inc(s_xl, 16)
                sp.wait_ge(s_tail, TSTEPS)
                sp.dma_start(out[last].rearrange("(k p) f -> p k f", p=P), lres).then_inc(s_xl, 16)
                sp.wait_ge(s_xl, 32)

            @block.gpsimd
            def _(pool):
                pool.sem_inc(s_fix, ONE)
                nc.gpsimd.memset(ident[:, :], 0.0).then_inc(s_id0, 1)
                nc.gpsimd.memset(identb[:, :], 0.0).then_inc(s_id0, 1)
                nc.gpsimd.memset(ones[:, :], 1.0).then_inc(s_const, 1)
                nc.gpsimd.memset(zerob[:, :], 0.0).then_inc(s_const, 1)
                nc.gpsimd.memset(Wx[:, :], 0.0).then_inc(s_const, 1)
                nc.gpsimd.memset(eps[:, :], EPS).then_inc(s_const, 1)
                nc.gpsimd.memset(tot[:, F:FE], float(N)).then_inc(s_const, 1)
                nc.gpsimd.memset(ext[:, 2:3], 0.0).then_inc(s_const, 1)
                pool.wait_ge(s_id0, 2)
                for m in (ident, identb):
                    nc.gpsimd.affine_select(out=m[:, :], in_=m[:, :], compare_op=ALU.not_equal, fill=1.0, base=0,
                                            pattern=[[-1, P]], channel_multiplier=1).then_inc(s_const, 1)
                pool.wait_ge(s_const, 8)
                pool.wait_ge(s_w, 48)
                nc.gpsimd.tensor_copy(Wx[0:F, 0:F], W2[0:F, :]).then_inc(s_Wcopy, 1)
                nc.gpsimd.tensor_copy(Wx[F:P, FX:FX + F], W2[F:P, :]).then_inc(s_Wcopy, 1)
                pool.wait_ge(s_us, 1)
                for r in range(QG):
                    b = slice(r * BU, (r + 1) * BU)
                    for h in range(2):
                        if r == 0 and h == 0:
                            continue
                        if r >= 2:
                            pool.wait_ge(s_lo[h], r - 1)
                        nc.gpsimd.tensor_tensor(Y[:, r % 2, h, :, 0:F], Wh[:, b, 0:F],
                                                uu[:, 2 + h, b].unsqueeze(2).to_broadcast([P, BU, F]), ALU.mult)
                        nc.gpsimd.tensor_copy(Y[:, r % 2, h, :, F], uu[:, 2 + h, b]).then_inc(s_Y[h], 1)
                for h in range(2):
                    pool.wait_ge(s_lo[h], QG)
                nc.gpsimd.tensor_tensor(tree[:, :, :], Wh[:, 0:JB // 2, 0:F], Wh[:, JB // 2:JB, 0:F],
                                        ALU.add).then_inc(s_tree, 1)
                w, n = JB // 4, 1
                while w >= 1:
                    pool.wait_ge(s_tree, n)
                    nc.gpsimd.tensor_tensor(tree[:, 0:w, :] if w > 1 else wh_sum[:, :].unsqueeze(1), tree[:, 0:w, :],
                                            tree[:, w:2 * w, :], ALU.add).then_inc(s_tree, 1)
                    w, n = w // 2, n + 1
                pool.wait_ge(s_ab, 1)
                nc.gpsimd.tensor_scalar(ab[:, :, :, 1], ab[:, :, :, 0], 1.0 / SPLIT, None, ALU.mult).then_inc(s_ab4, 1)
                pool.wait_ge(s_ab4, 1)
                for c in range(2 * (G - 1)):

                    def after(k):
                        pool.wait_ge(s_fix, ONE + c * STEPS + k)

                    pool.dma_start(xg[:, :, :], x_v[c]).then_inc(s_xg, 16)
                    for v in s_evac:
                        pool.wait_ge(v, ONE + c // 2 + 1)
                    mine = acc_sb[:, c % 2 * KE * 2 * FP:(c % 2 + 1) * KE * 2 * FP]
                    acc_v = mine.rearrange("p (k f) -> p k f", f=FE)
                    nc.gpsimd.tensor_tensor(acc_v, acc_v, ab[:, c * KE:(c + 1) * KE].rearrange("p k s h -> p (k s h)")
                                            .unsqueeze(2).to_broadcast([P, 4 * KE, FE]), ALU.mult).then_inc(s_fix, 1)
                    after(1)
                    acc_h = mine.rearrange("p (k h f) -> p k h f", h=2, f=FE)
                    nc.gpsimd.tensor_tensor(parts[:, :, :, :].rearrange("p k s f -> p (k s) f"), acc_h[:, :, 0],
                                            acc_h[:, :, 1], ALU.add).then_inc(s_fix, 1)
                    after(2)
                    nc.gpsimd.tensor_tensor(sums[:, :, :], parts[:, :, 0], parts[:, :, 1], ALU.add).then_inc(s_fix, 1)
                    after(3)
                    nc.gpsimd.tensor_scalar(lone[:, :], sums[:, :, F], 0.0, None, ALU.is_equal).then_inc(s_fix, 1)
                    after(4)
                    nc.gpsimd.tensor_tensor(fixd[:, :, :], lone[:, :].unsqueeze(2).to_broadcast([P, KE, FE]),
                                            tot[:, :].unsqueeze(1).to_broadcast([P, KE, FE]), ALU.mult)\
                        .then_inc(s_fix, 1)
                    after(5)
                    nc.gpsimd.tensor_tensor(fixd[:, :, :], fixd[:, :, :], sums[:, :, :], ALU.add).then_inc(s_fix, 1)
                    pool.wait_ge(s_rden, c + 1)
                    nc.gpsimd.tensor_tensor(hp[:, :, :], fixd[:, :, 0:F],
                                            rden[:, :].unsqueeze(2).to_broadcast([P, KE, F]), ALU.mult).then_inc(s_fix, 1)
                    after(7)
                    nc.gpsimd.tensor_scalar(neg[:, :, :], hp[:, :, :], 0.0, None, ALU.min).then_inc(s_neg, 1)
                    nc.gpsimd.tensor_scalar(hp[:, :, :], hp[:, :, :], 0.0, -1.0, ALU.max, ALU.add).then_inc(s_fix, 1)
                    after(8)
                    pool.wait_ge(s_xg, 16 * c + 16)
                    nc.gpsimd.tensor_tensor(hp[:, :, :], hp[:, :, :], xg[:, :, :], ALU.add).then_inc(s_fix, 1)
                    after(STEPS)
                    pool.wait_ge(s_exp, c + 1)
                    if c:
                        pool.wait_ge(s_out, 16 * c)
                    nc.gpsimd.tensor_tensor(res[:, :, :], hp[:, :, :], neg[:, :, :], ALU.add).then_inc(s_res, 1)
                    pool.wait_ge(s_res, c + 1)
                    pool.dma_start(out_v[c], res[:, :, :]).then_inc(s_out, 16)
                pool.wait_ge(s_out, 16 * 2 * (G - 1))

            @block.scalar
            def _(act):
                for v in s_san:
                    act.sem_inc(v, ONE)
                for v in s_evac[:NA // 2]:
                    act.sem_inc(v, ONE)
                for h in range(2):
                    act.dma_start(W2[h * F:(h + 1) * F, :], W).then_inc(s_w, 16)
                with nc.allow_non_contiguous_dma(reason="128 numbers"):
                    act.dma_start(a_sb[:, :], a.rearrange("(c f) o -> f (c o)", c=2)).then_inc(s_w, 16)

                def squares(b):
                    r = slice(b * RR, (b + 1) * RR)
                    act.wait_ge(s_xc, b + 1)
                    nc.scalar.activation(sq[:, r], xh[:, r], ACT.Square).then_inc(s_sq, 1)

                def copy_hT(b):
                    act.wait_ge(s_hT, b + 1)
                    nc.scalar.activation(hT[:, b * PR * P:(b + 1) * PR * P].rearrange("p (b w) -> p b w", b=2),
                                         hT_ps[b % 2], ACT.Relu).then_inc(s_hTc, 1)

                def deviation(b):
                    r = slice(b * RR, (b + 1) * RR)
                    act.wait_ge(s_var, b + 1)
                    nc.scalar.activation(stat[:, 3, r], stat[:, 2, r], ACT.Sqrt, bias=eps[:, :],
                                         scale=1.0 / F).then_inc(s_std, 1)

                act.wait_ge(s_wp, 1)
                nc.scalar.activation(WT[:, :], psum[0:F, 7, 0:P], ACT.Copy).then_inc(s_wt, 1)
                squares(0)
                act.wait_ge(s_wp, 2)
                act.wait_ge(s_Wcopy, 2)
                nc.scalar.activation(Wx[0:F, F:FX], psum[0:F, 7, P:P + 2], ACT.Copy).then_inc(s_wx, 1)
                nc.scalar.activation(Wx[F:P, FX + F:2 * FX], psum[F:P, 7, P:P + 2], ACT.Copy).then_inc(s_wx, 1)
                copy_hT(0)
                act.wait_ge(s_const, 8)
                for b in range(1, NR):
                    squares(b)
                    deviation(b - 1)
                    copy_hT(b)
                deviation(NR - 1)
                act.wait_ge(s_norm, 2)
                nc.scalar.activation(ext[0:F, 2:3], norm2[:, :], ACT.Sqrt, scale=float(F)).then_inc(s_sq2, 1)
                act.wait_ge(s_sTp, 1)
                nc.scalar.activation(sT[:, :], psum[0:JB, 1, 0:P], ACT.Copy).then_inc(s_sT, 1)
                act.wait_ge(s_lim, 1)
                t_all = Wh[:, :, F + 1]
                nc.scalar.activation(uu[:, 0], t_all, ACT.Exp, bias=lim[:, 3:4]).then_inc(s_u, 1)
                nc.scalar.activation(uu[:, 1], t_all, ACT.Exp, bias=lim[:, 4:5], scale=ALPHA).then_inc(s_u, 1)
                nc.scalar.activation(bt[:, :], t_all, ACT.Copy, scale=BIG).then_inc(s_small, 1)

                def high_parts(r):
                    b = slice(r * BU, (r + 1) * BU)
                    for h in range(2):
                        if r == 0 and h == 0:
                            act.wait_ge(s_Y0, 1)
                        else:
                            act.wait_ge(s_Y[h], r + h)
                        nc.scalar.activation(V[:, b, 2 * h * FP:2 * h * FP + FE], Y[:, r % 2, h], ACT.Copy,
                                             scale=1.0 / SPLIT).then_inc(s_hi[h], 1)

                high_parts(0)
                act.wait_ge(s_yy, 2)
                nc.scalar.activation(ab[:, :, :, 0], yy[:, :, :], ACT.Exp).then_inc(s_ab, 1)
                nc.scalar.activation(umin[:, :], lim[:, 1:2], ACT.Exp, bias=lim[:, 3:4], scale=-1.0)\
                    .then_inc(s_umin, 1)

                def prepare(m, g, q, parts_of=None):
                    for s in range(RC):
                        mine = [u for u in range(UC * s, UC * (s + 1)) if u in AS]
                        if mine:
                            act.wait_ge(s_up, m * BU + mine[-1] + 1)
                        act.wait_ge(s_adj[s], 16 * m + 16)
                        act.wait_ge(s_T[UC * s + UC - 1], ONE + m)
                        nc.scalar.activation(san[:, s], adj_ring[:, s], ACT.Relu).then_inc(s_san[s], 1)
                        for u in mine:
                            nc.scalar.activation(step[:, u], srow[:, bass.ds(g * WI, WI)], ACT.Relu,
                                                 bias=bt[:, bass.ds(q * BU + u, 1)], scale=BIG).then_inc(s_stepA, 1)
                        if s == 1 and parts_of is not None:
                            high_parts(parts_of)

                def copy_sums(g):
                    act.wait_ge(s_group, g + 1)
                    act.wait_ge(s_fix, ONE + g * 2 * STEPS)
                    for b in range(NA // 2):
                        nc.scalar.activation(acc_sb[:, b * NS * FP:(b + 1) * NS * FP], sum_bank[b][:, 0:NS * FP],
                                             ACT.Copy).then_inc(s_evac[b], 1)

                def exp_part(c):
                    act.wait_ge(s_neg, c + 1)
                    nc.scalar.activation(neg[:, :, :], neg[:, :, :], ACT.Exp).then_inc(s_exp, 1)

                act.wait_ge(s_var, NR)
                act.wait_ge(s_small, 1)
                act.wait_ge(s_hT, NR)
                act.wait_ge(s_srow0, 16)
                for q in range(QG):
                    prepare(q, 0, q, parts_of=q + 1 if q + 1 < QG else None)
                act.wait_ge(s_srow, 16)
                with act.Fori(0, G - 1) as g:
                    prepare((g + 1) * QG, g + 1, 0)
                    copy_sums(g)
                    with act.Fori(1, 4) as q:
                        prepare((g + 1) * QG + q, g + 1, q)
                    exp_part(2 * g)
                    with act.Fori(4, 6) as q:
                        prepare((g + 1) * QG + q, g + 1, q)
                    exp_part(2 * g + 1)
                    with act.Fori(6, QG) as q:
                        prepare((g + 1) * QG + q, g + 1, q)
                copy_sums(G - 1)
                act.wait_ge(s_tail, 9)
                nc.scalar.activation(lneg, lneg, ACT.Exp).then_inc(s_lneg, 1)

            @block.vector
            def _(dve):
                dve.sem_inc(s_mask, TB)
                for v in s_evac[NA // 2:]:
                    dve.sem_inc(v, ONE)
                dve.sem_inc(s_up, BU)

                def centre(b):
                    r = slice(b * RR, (b + 1) * RR)
                    dve.wait_ge(s_x[b], 16)
                    nc.vector.reduce_sum(stat[:, 0, r], xh[:, r], axis=AX.X).then_inc(s_sum, 1)
                    dve.wait_ge(s_sum, b + 1)
                    nc.vector.tensor_scalar(stat[:, 1, r], stat[:, 0, r], -1.0 / F, None, ALU.mult).then_inc(s_nm, 1)
                    dve.wait_ge(s_nm, b + 1)
                    nc.vector.tensor_tensor(xh[:, r], xh[:, r], stat[:, 1, r].unsqueeze(2).to_broadcast([P, RR, F]),
                                            ALU.add).then_inc(s_xc, 1)

                def variance(b):
                    r = slice(b * RR, (b + 1) * RR)
                    dve.wait_ge(s_sq, b + 1)
                    nc.vector.reduce_sum(stat[:, 2, r], sq[:, r], axis=AX.X).then_inc(s_var, 1)

                def copy_Wh(b):
                    r = slice(b * RR, (b + 1) * RR)
                    dve.wait_ge(s_std, b + 1)
                    nc.vector.reciprocal(stat[:, 4, r], stat[:, 3, r]).then_inc(s_rstd, 1)
                    dve.wait_ge(s_rstd, b + 1)
                    for i in range(2):
                        r = slice(b * RR + i * 2 * HP, b * RR + (i + 1) * 2 * HP)
                        dve.wait_ge(s_Wh, 2 * b + i + 1)
                        nc.vector.tensor_tensor(Wh[:, r, :].rearrange("p (b j) f -> p b j f", b=2),
                                                Wh_ps[i][:, :, 0:HP * FX].rearrange("p b (j f) -> p b j f", f=FX),
                                                stat[:, 4, r].rearrange("p (b j) -> p b j", b=2).unsqueeze(3)
                                                .to_broadcast([P, 2, HP, FX]), ALU.mult).then_inc(s_Whc, 1)

                centre(0)
                centre(1)
                variance(0)
                centre(2)
                variance(1)
                copy_Wh(0)
                centre(3)
                variance(2)
                copy_Wh(1)
                variance(3)
                dve.wait_ge(s_wt, 1)
                nc.vector.tensor_tensor(WT2[:, :], WT[:, 0:F], WT[:, 0:F], ALU.mult).then_inc(s_norm, 1)
                dve.wait_ge(s_norm, 1)
                nc.vector.reduce_sum(norm2[:, :], WT2[:, :], axis=AX.X).then_inc(s_norm, 1)
                copy_Wh(2)
                copy_Wh(3)
                dve.wait_ge(s_Whc, 2 * NR)
                t_all = Wh[:, :, F + 1]
                nc.vector.tensor_reduce(ext[:, 0:1], t_all, AX.X, ALU.max).then_inc(s_ext, 1)
                nc.vector.tensor_reduce(ext[:, 1:2], t_all, AX.X, ALU.min).then_inc(s_ext, 1)
                dve.wait_ge(s_ext, 2)
                nc.vector.tensor_scalar(ext[:, 1:2], ext[:, 1:2], -1.0, None, ALU.mult).then_inc(s_ext, 1)
                dve.wait_ge(s_extp, 1)
                nc.vector.tensor_reduce(ext2[:, 0:1], psum[0:3, 0, 0:P], AX.X, ALU.max).then_inc(s_ext, 1)
                dve.wait_ge(s_ext, 4)
                nc.vector.tensor_scalar(extd[:, :], ident[0:3, 0:3], ext2[:, 0:1], None, ALU.mult).then_inc(s_ext, 1)
                dve.wait_ge(s_extp, 2)
                nc.vector.tensor_copy(lim[:, 0:3], psum[:, 0, P:P + 3]).then_inc(s_ext, 1)
                dve.wait_ge(s_ext, 6)
                nc.vector.tensor_scalar(lim[:, 3:4], lim[:, 0:1], -1.0, None, ALU.mult)
                nc.vector.tensor_scalar(lim[:, 4:5], lim[:, 0:1], -ALPHA, None, ALU.mult)
                nc.vector.tensor_scalar(lim[:, 5:6], lim[:, 2:3], 1.0, 1.0 / (TOP * SPLIT), ALU.max,
                                        ALU.mult).then_inc(s_lim, 1)
                dve.wait_ge(s_lim, 1)
                nc.vector.reciprocal(lim[:, 6:7], lim[:, 5:6]).then_inc(s_lim, 1)
                dve.wait_ge(s_u, 2)
                dve.wait_ge(s_lim, 2)
                nc.vector.tensor_scalar(uu[:, 2:4], uu[:, 0:2], lim[:, 6:7], None, ALU.mult).then_inc(s_us, 1)
                dve.wait_ge(s_us, 1)
                r = slice(0, BU)
                nc.vector.tensor_tensor(Y[:, 0, 0, :, 0:F], Wh[:, r, 0:F],
                                        uu[:, 2, r].unsqueeze(2).to_broadcast([P, BU, F]), ALU.mult)
                nc.vector.tensor_copy(Y[:, 0, 0, :, F], uu[:, 2, r]).then_inc(s_Y0, 1)

                def low_parts(r):
                    b = slice(r * BU, (r + 1) * BU)
                    for h in range(2):
                        o = 2 * h * FP
                        dve.wait_ge(s_hi[h], r + 1)
                        nc.vector.scalar_tensor_tensor(out=V[:, b, o + FE:o + FP], in0=V[:, b, o:o + FE],
                                                       scalar=-SPLIT, in1=Y[:, r % 2, h], op0=ALU.mult, op1=ALU.add)\
                            .then_inc(s_lo[h], 1)
                    dve.wait_ge(s_lo[1], r + 1)
                    nc.vector.tensor_scalar(V[:, b, FP:2 * FP], V[:, b, 2 * FP:3 * FP], -1.0, None,
                                            ALU.mult).then_inc(s_V, 1)

                s_all = Wh[:, :, F]
                nc.vector.tensor_scalar(yy[:, :, 0], s_all, lim[:, 0:1], 1 - ALPHA, ALU.add, ALU.mult).then_inc(s_yy, 1)
                dve.wait_ge(s_yy, 1)
                nc.vector.tensor_scalar(yy[:, :, 1], yy[:, :, 0], -1.0, 0.0, ALU.mult, ALU.min).then_inc(s_ext, 1)
                dve.wait_ge(s_ext, 7)
                nc.vector.tensor_scalar(yy[:, :, 0], yy[:, :, 0], 0.0, None, ALU.min).then_inc(s_yy, 1)
                nc.vector.tensor_scalar(nt[:, :], Wh[:, :, F + 1], -1.0, None, ALU.mult).then_inc(s_ext, 1)
                low_parts(0)
                dve.wait_ge(s_umin, 1)
                nc.vector.tensor_scalar(flag[:, :], umin[:, :], lim[:, 6:7], LEAST * SPLIT, ALU.mult, ALU.is_lt)\
                    .then_inc(s_flag, 1)
                dve.wait_ge(s_srow0, 16)
                dve.wait_ge(s_ext, 8)
                dve.wait_ge(s_hT, NR)

                def take_up(m, u):
                    dve.wait_ge(s_mask, TB + m * BU + u + 1)
                    if u in AS:
                        dve.wait_ge(s_stepA, m * len(AS) + AS.index(u) + 1)
                    else:
                        dve.wait_ge(s_stepV, m * len(VS) + VS.index(u) + 1)
                    nc.vector.tensor_tensor(up[:, u % RU], mask[:, u % RU], step[:, u], ALU.min).then_inc(s_up, 1)

                def take_down(m, u):
                    dve.wait_ge(s_up, BU + m * BU + u + 1)
                    nc.vector.tensor_tensor(mask[:, u % RU], mask[:, u % RU], up[:, u % RU],
                                            ALU.subtract).then_inc(s_down, 1)

                def mask_unit(m, g, q, u):
                    dve.wait_ge(s_T[u], ONE + m + 1)
                    dve.wait_ge(s_P[u % RU], ONE + m * (BU // RU) + u // RU)
                    nc.vector.tensor_scalar(mask[:, u % RU], adjT[u % TB], 0.0, None, ALU.is_gt).then_inc(s_mask, 1)
                    if u - 2 in DN:
                        take_down(m, u - 2)
                    if u in VS:
                        dve.wait_ge(s_up, m * BU + u + 1)
                        nc.vector.tensor_scalar(step[:, u], srow[:, bass.ds(g * WI, WI)],
                                                nt[:, bass.ds(q * BU + u, 1)], None, ALU.is_ge).then_inc(s_stepV, 1)
                    if u:
                        take_up(m, u - 1)

                def copy_sums(g):
                    dve.wait_ge(s_group, g + 1)
                    dve.wait_ge(s_fix, ONE + g * 2 * STEPS)
                    for b in range(NA // 2, NA):
                        w = min(NS * FP, 2 * K * FP - b * NS * FP)
                        nc.vector.tensor_copy(acc_sb[:, b * NS * FP:b * NS * FP + w], sum_bank[b][:, 0:w])\
                            .then_inc(s_evac[b], 1)
                    nc.vector.tensor_copy(tot[:, 0:F], total_ps).then_inc(s_evac[NA], 1)

                def masks(g, first, bodies):
                    with dve.Fori(first, first + bodies) as q:
                        for u in range(BU):
                            mask_unit(g * QG + q, g, q, u)
                        take_up(g * QG + q, BU - 1)

                def invert(c):
                    dve.wait_ge(s_fix, ONE + c * STEPS + 6)
                    nc.vector.reciprocal(rden[:, :], fixd[:, :, F]).then_inc(s_rden, 1)

                for q in range(QG):
                    for u in range(BU):
                        mask_unit(q, 0, q, u)
                    if q + 1 < QG:
                        low_parts(q + 1)
                    take_up(q, BU - 1)
                dve.wait_ge(s_srow, 16)
                with dve.Fori(0, G - 1) as g:
                    for u in range(BU):
                        if u == LEAD:
                            copy_sums(g)
                        mask_unit((g + 1) * QG, g + 1, 0, u)
                    take_up((g + 1) * QG, BU - 1)
                    masks(g + 1, 1, 1)
                    invert(2 * g)
                    masks(g + 1, 2, 2)
                    invert(2 * g + 1)
                    masks(g + 1, 4, QG - 4)
                copy_sums(G - 1)

                def after(k):
                    dve.wait_ge(s_tail, k)

                for v in s_evac:
                    dve.wait_ge(v, ONE + G)
                dve.wait_ge(s_xl, 16)
                last = slice((G - 1) * K, G * K)
                acc_v = acc_sb.rearrange("p (k f) -> p k f", f=FE)
                nc.vector.tensor_tensor(acc_v, acc_v, ab[:, last].rearrange("p k s h -> p (k s h)").unsqueeze(2)
                                        .to_broadcast([P, 4 * K, FE]), ALU.mult).then_inc(s_tail, 1)
                after(1)
                acc_h = acc_sb.rearrange("p (k h f) -> p k h f", h=2, f=FE)
                nc.vector.tensor_tensor(lparts, acc_h[:, :, 0], acc_h[:, :, 1], ALU.add).then_inc(s_tail, 1)
                after(2)
                lparts_s = lparts.rearrange("p (k s) f -> p k s f", s=2)
                nc.vector.tensor_tensor(lsum, lparts_s[:, :, 0], lparts_s[:, :, 1], ALU.add).then_inc(s_tail, 1)
                after(3)
                nc.vector.tensor_scalar(llone, lsum[:, :, F], 0.0, None, ALU.is_equal).then_inc(s_tail, 1)
                after(4)
                nc.vector.tensor_tensor(lfix, llone.unsqueeze(2).to_broadcast([P, K, FE]),
                                        tot[:, :].unsqueeze(1).to_broadcast([P, K, FE]), ALU.mult).then_inc(s_tail, 1)
                after(5)
                nc.vector.tensor_tensor(lfix, lfix, lsum, ALU.add).then_inc(s_tail, 1)
                after(6)
                nc.vector.reciprocal(lrden, lfix[:, :, F]).then_inc(s_tail, 1)
                after(7)
                nc.vector.tensor_tensor(lhp, lfix[:, :, 0:F], lrden.unsqueeze(2).to_broadcast([P, K, F]),
                                        ALU.mult).then_inc(s_tail, 1)
                after(8)
                nc.vector.tensor_scalar(lneg, lhp, 0.0, None, ALU.min).then_inc(s_tail, 1)
                nc.vector.scalar_tensor_tensor(out=lhp, in0=lhp, scalar=0.0, in1=lx, op0=ALU.max,
                                               op1=ALU.add).then_inc(s_tail, 1)
                after(10)
                dve.wait_ge(s_lneg, 1)
                nc.vector.scalar_tensor_tensor(out=lres, in0=lneg, scalar=-1.0, in1=lhp, op0=ALU.add,
                                               op1=ALU.add).then_inc(s_tail, 1)

            @block.tensor
            def _(pe):
                for v in s_T + s_P:
                    pe.sem_inc(v, ONE)
                pe.wait_ge(s_w, 48)
                pe.wait_ge(s_const, 8)
                nc.tensor.transpose(psum[0:F, 7, 0:P], W2[:, :], ident[:, :]).then_inc(s_wp, 1)
                pe.wait_ge(s_wt, 1)
                nc.tensor.matmul(psum[:, 7, P:P + 2], WT[:, :], a_sb[:, :], start=True, stop=True).then_inc(s_wp, 1)

                def transpose_round(b):
                    pe.wait_ge(s_xc, b + 1)
                    if b >= 2:
                        pe.wait_ge(s_hTc, b - 1)
                    for c in range(PR):
                        r = 2 * (b * PR + c)
                        last = nc.tensor.transpose(hT_ps[b % 2][:, c // 4, (c % 4) * P:(c % 4 + 1) * P],
                                                   xh[:, r:r + 2, :].rearrange("p r f -> p (r f)"), ident[:, :])
                    last.then_inc(s_hT, 1)

                def Wh_half_rounds(b):
                    pe.wait_ge(s_hTc, b + 1)
                    for i in range(2):
                        if b:
                            pe.wait_ge(s_Whc, 2 * b + i - 1)
                        for c in range(HP):
                            last = nc.tensor.matmul(Wh_ps[i][:, c // (HP // 2), (c % (HP // 2)) * 2 * FX:
                                                             (c % (HP // 2) + 1) * 2 * FX],
                                                    pair(b * PR + i * HP + c), Wx[:, :], start=True, stop=True)
                        last.then_inc(s_Wh, 1)

                transpose_round(0)
                pe.wait_ge(s_wx, 2)
                for b in range(NR):
                    if b + 1 < NR:
                        transpose_round(b + 1)
                    Wh_half_rounds(b)
                pe.wait_ge(s_Whc, 2 * NR)
                nc.tensor.transpose(psum[0:JB, 1, 0:P], Wh[:, :, F], ident[:, :]).then_inc(s_sTp, 1)
                pe.wait_ge(s_ext, 3)
                pe.wait_ge(s_sq2, 1)
                nc.tensor.transpose(psum[0:3, 0, 0:P], ext[:, :], ident[:, :]).then_inc(s_extp, 1)
                pe.wait_ge(s_ext, 5)
                nc.tensor.matmul(psum[:, 0, P:P + 3], ones[0:3, :], extd[:, :], start=True, stop=True)\
                    .then_inc(s_extp, 1)

                def transpose_unit(m, u):
                    if u % UC == 0:
                        pe.wait_ge(s_san[u // UC], ONE + m + 1)
                    pe.wait_ge(s_mask, m * BU + u + 1)
                    for k in range(K):
                        c = u % UC
                        last = nc.tensor.transpose(adjT[u % TB][:, k * P:(k + 1) * P],
                                                   san[:, u // UC, k, c * P:(c + 1) * P], identb[:, :])
                    last.then_inc(s_T[u], 1)

                def add_to_sums(i, n, edges, values):
                    done = 0
                    while done < n:
                        b, c = (i + done) // NS, (i + done) % NS
                        w = min(n - done, NS - c)
                        inst = nc.tensor.matmul(sum_bank[b][:, c * FP:(c + w) * FP], edges,
                                                values[:, done * FP:(done + w) * FP], start=False, stop=False,
                                                skip_group_check=True)
                        done += w
                    return inst

                def multiply_unit(m, u, q):
                    if u == 0:
                        pe.wait_ge(s_V, q + 1)
                    if u in DN:
                        pe.wait_ge(s_down, m * len(DN) + DN.index(u) + 1)
                    else:
                        pe.wait_ge(s_up, BU + m * BU + u + 1)
                    v = V[:, bass.ds(q * BU + u, 1), :].rearrange("p o v -> p (o v)")
                    for k in range(K):
                        mask_k = mask[:, u % RU, k * P:(k + 1) * P]
                        up_k = up[:, u % RU, k * P:(k + 1) * P]
                        add_to_sums(2 * k + 1, 1, mask_k, v[:, 2 * FP:3 * FP])
                        last = add_to_sums(2 * k, 1 if u in DN else 2, up_k, v[:, 0:2 * FP])
                    last.then_inc(s_P[u % RU], 1)

                def body(m, q, last=False):
                    for u in range(BU):
                        if u + LEAD < BU:
                            transpose_unit(m, u + LEAD)
                        elif not last:
                            transpose_unit(m + 1, u + LEAD - BU)
                        multiply_unit(m, u, q)

                def open_group(g):
                    for b in range(NA):
                        pe.wait_ge(s_evac[b], ONE + g)
                        if b == NA - 1:
                            pe.wait_ge(s_evac[NA], ONE + g)
                        nc.tensor.matmul(sum_bank[b][:, 0:NS * FP], identb[:, :], zerob[:, :], start=True, stop=False,
                                         skip_group_check=True)

                def close_group():
                    pe.wait_ge(s_tree, 6)
                    nc.tensor.matmul(total_ps, ones[:, :], wh_sum[:, :], start=False, stop=True,
                                     skip_group_check=True).then_inc(s_group, 1)

                pe.wait_ge(s_lim, 1)
                pe.wait_ge(s_sT, 1)
                for u in range(LEAD):
                    transpose_unit(0, u)
                with pe.Fori(0, G - 1) as g:
                    open_group(g)
                    with pe.Fori(0, QG) as q:
                        body(g * QG + q, q)
                    close_group()
                open_group(G - 1)
                with pe.Fori(0, QG - 1) as q:
                    body((G - 1) * QG + q, q)
                body(G * QG - 1, QG - 1, last=True)
                close_group()

        A = adj_ring[:, :, :, :].rearrange("p s k j -> p (s k j)")
        score = flat
        trow = srow
        whole = V[:, :, :].rearrange("p j v -> p (j v)").bitcast(F32)
        Wh1 = whole[:, 0:JB * FE].rearrange("p (j f) -> p j f", f=FE)
        probT = whole[:, JB * FE:JB * FE + N]
        xt, hpt, negt, rest = xg[:, 0], hp[:, 0], neg[:, 0], res[:, 0]
        rdent, rowmax = rden[:, 0:1], lone[:, 0:1]
        acc1 = psum[:, 0, 0:FE]
        Q = N // NR
        DSTEPS = 9

        def trow_round(r):
            return trow[:, r * Q:(r + 1) * Q].rearrange("q (b w) -> q b w", b=4), half[r % 2]

        def probT_round(r):
            return probT[:, r * Q:(r + 1) * Q].rearrange("q (b w) -> q b w", b=4), half[r % 2]

        g_adj = sem("general_adj_loaded")
        g_x = sem("general_x_loaded")
        g_read = sem("general_adj_read")
        g_dve = sem("general_step_of_VectorE")
        g_round = sem("general_round_in_psum")
        g_even = sem("general_even_round_copied")
        g_odd = sem("general_odd_round_copied")
        g_prob = sem("general_probabilities_ready")
        g_acc = sem("general_rows_summed")
        g_fin = sem("general_last_steps")
        g_neg = sem("general_negative_part_exp")
        g_res = sem("general_result_ready")
        g_out = sem("general_out_stored")

        def needed(engine):
            return engine.value_load(flag[0:1, 0:1], min_val=0, max_val=1) != 0

        with nc.Block() as general:

            @general.sync
            def _(sp):
                with sp.If(needed(sp)):
                    sp.sem_inc(g_out, ONE)
                    with sp.Fori(0, JB) as i:
                        sp.wait_ge(g_read, ONE + i)
                        sp.dma_start(A, adj[bass.ds(i * P, P), :]).then_inc(g_adj, 16)
                        sp.wait_ge(g_res, ONE + i)
                        sp.dma_start(xt, x[bass.ds(i * P, P), :]).then_inc(g_x, 16)

            @general.scalar
            def _(act):
                with act.If(needed(act)):
                    for r in (1, 3):
                        act.wait_ge(g_round, r + 1)
                        nc.scalar.activation(*trow_round(r), ACT.Copy).then_inc(g_odd, 1)
                    with act.Fori(0, JB) as i:
                        act.wait_ge(g_dve, i * DSTEPS + 6)
                        for r in range(NR):
                            nc.scalar.activation(score[:, r * Q:(r + 1) * Q], score[:, r * Q:(r + 1) * Q], ACT.Exp,
                                                 bias=rowmax).then_inc(g_prob, 1)
                        for r in (1, 3):
                            act.wait_ge(g_round, NR + i * NR + r + 1)
                            nc.scalar.activation(*probT_round(r), ACT.Copy).then_inc(g_odd, 1)
                        act.wait_ge(g_dve, i * DSTEPS + 9)
                        nc.scalar.activation(negt, negt, ACT.Exp).then_inc(g_neg, 1)
                        act.wait_ge(g_res, ONE + i + 1)
                        act.dma_start(out[bass.ds(i * P, P), :], rest).then_inc(g_out, 16)
                    act.wait_ge(g_out, ONE + 16 * JB)

            @general.vector
            def _(dve):
                with dve.If(needed(dve)):
                    dve.sem_inc(g_read, ONE)
                    dve.sem_inc(g_res, ONE)
                    for r in (0, 2):
                        dve.wait_ge(g_round, r + 1)
                        nc.vector.tensor_copy(*trow_round(r)).then_inc(g_even, 1)
                    nc.vector.tensor_copy(Wh1[:, :, 0:F], Wh[:, :, 0:F]).then_inc(g_even, 1)
                    nc.vector.memset(Wh1[:, :, F:FE], 1.0).then_inc(g_even, 1)
                    dve.wait_ge(g_even, 2)
                    dve.wait_ge(g_odd, 2)
                    with dve.Fori(0, JB) as i:

                        def after(k):
                            dve.wait_ge(g_dve, i * DSTEPS + k)

                        dve.wait_ge(g_adj, 16 * i + 16)
                        nc.vector.tensor_scalar(score, A, 0.0, None, ALU.is_gt).then_inc(g_read, 1)
                        dve.wait_ge(g_read, ONE + i + 1)
                        nc.vector.tensor_scalar(score, score, -1.0, -MASKED, ALU.add, ALU.mult).then_inc(g_dve, 1)
                        after(1)
                        nc.vector.tensor_tensor(score, score, trow[:, :], ALU.add).then_inc(g_dve, 1)
                        after(2)
                        nc.vector.tensor_scalar(score, score, Wh[:, bass.ds(i, 1), F], None, ALU.add)\
                            .then_inc(g_dve, 1)
                        after(3)
                        nc.vector.scalar_tensor_tensor(out=score, in0=score, scalar=ALPHA, in1=score, op0=ALU.mult,
                                                       op1=ALU.max).then_inc(g_dve, 1)
                        after(4)
                        nc.vector.tensor_reduce(rowmax, score, AX.X, ALU.max).then_inc(g_dve, 1)
                        after(5)
                        nc.vector.tensor_scalar(rowmax, rowmax, -1.0, None, ALU.mult).then_inc(g_dve, 1)
                        for r in (0, 2):
                            dve.wait_ge(g_round, NR + i * NR + r + 1)
                            nc.vector.tensor_copy(*probT_round(r)).then_inc(g_even, 1)
                        dve.wait_ge(g_acc, i + 1)
                        nc.vector.reciprocal(rdent, acc1[:, F:FE]).then_inc(g_dve, 1)
                        after(7)
                        nc.vector.tensor_scalar(hpt, acc1[:, 0:F], rdent, None, ALU.mult).then_inc(g_dve, 1)
                        after(8)
                        nc.vector.tensor_scalar(negt, hpt, 0.0, None, ALU.min).then_inc(g_dve, 1)
                        dve.wait_ge(g_neg, i + 1)
                        nc.vector.tensor_scalar(hpt, hpt, 0.0, -1.0, ALU.max, ALU.add).then_inc(g_fin, 1)
                        dve.wait_ge(g_fin, 2 * i + 1)
                        nc.vector.tensor_tensor(hpt, hpt, negt, ALU.add).then_inc(g_fin, 1)
                        dve.wait_ge(g_fin, 2 * i + 2)
                        dve.wait_ge(g_x, 16 * i + 16)
                        dve.wait_ge(g_out, ONE + 16 * i)
                        nc.vector.tensor_tensor(rest, hpt, xt, ALU.add).then_inc(g_res, 1)

            @general.tensor
            def _(pe):
                with pe.If(needed(pe)):
                    for r in range(NR):
                        if r >= 2:
                            pe.wait_ge(g_even if r % 2 == 0 else g_odd, r // 2)
                        for j in range(RR):
                            jb = r * RR + j
                            last = nc.tensor.transpose(half[r % 2][:, j // 4, (j % 4) * P:(j % 4 + 1) * P],
                                                       Wh[:, jb, F + 1:FX].to_broadcast([P, P]), ident[:, :])
                        last.then_inc(g_round, 1)
                    pe.wait_ge(g_even, 4)
                    pe.wait_ge(g_odd, 2)
                    with pe.Fori(0, JB) as i:
                        pe.wait_ge(g_res, ONE + i)
                        for r in range(NR):
                            pe.wait_ge(g_prob, i * NR + r + 1)
                            if r >= 2:
                                pe.wait_ge(g_even if r % 2 == 0 else g_odd, (4 if r % 2 == 0 else 2) + 2 * i + r // 2)
                            for j in range(RR):
                                jb = r * RR + j
                                last = nc.tensor.transpose(half[r % 2][:, j // 4, (j % 4) * P:(j % 4 + 1) * P],
                                                           score[:, jb * P:(jb + 1) * P], ident[:, :])
                            last.then_inc(g_round, 1)
                        pe.wait_ge(g_even, 4 + 2 * i + 2)
                        pe.wait_ge(g_odd, 2 + 2 * i + 2)
                        for jb in range(JB):
                            last = nc.tensor.matmul(acc1, probT[:, jb * P:(jb + 1) * P], Wh1[:, jb, :],
                                                    start=jb == 0, stop=jb == JB - 1)
                        last.then_inc(g_acc, 1)


_INS = ["x", "adj", "L0_gnn_W", "L0_gnn_a"]


def kernel(**inputs):
    import numpy as np
    import concourse.bacc as bacc
    from concourse.bass_utils import run_bass_kernel_spmd

    nc = bacc.Bacc("TRN2", target_bir_lowering=False, num_devices=1)
    arrays, args = {}, []
    for name in _INS:
        v = np.ascontiguousarray(inputs[name])
        arrays[f"in_{name}"] = v
        args.append(nc.dram_tensor(f"in_{name}", v.shape, mybir.dt.from_np(v.dtype), kind="ExternalInput").ap())
    y = nc.dram_tensor("out_y", arrays["in_x"].shape, F32, kind="ExternalOutput").ap()
    s_nodes = nc.dram_tensor("s_nodes", [arrays["in_x"].shape[0]], F32, kind="Internal").ap()
    build_gat(nc, *args, y, s_nodes)
    r = run_bass_kernel_spmd(nc, [arrays], core_ids=[0])
    return r.results[0]["out_y"]
```
